# Optimizing a Trainium2 kernel written in Bass

```python
import numpy as np
import jax
import jax.numpy as jnp

def _softmax(x, axis=-1):
    return jax.nn.softmax(x, axis=axis)

def _gelu(x):
    return jax.nn.gelu(x, approximate=True)

def _silu(x):
    return jax.nn.silu(x)

def _sigmoid(x):
    return jax.nn.sigmoid(x)

def _layernorm(x, axis=-1, eps=1e-05):
    m = jnp.mean(x, axis=axis, keepdims=True)
    v = jnp.var(x, axis=axis, keepdims=True)
    return (x - m) / jnp.sqrt(v + eps)

def _scatter_add(tgt, idx, src, axis=0):
    return tgt.at[idx].add(src)

def _segment_sum(src, seg, n):
    return jax.ops.segment_sum(src, seg, n)
kernel_name = 'mk_prb_d1_jaxref_r8_a38ae7'

def setup_inputs(seed: int=0):
    np.random.seed(seed)
    _w = jnp.asarray

    def _L0_attn_setup():
        import jax, jax.numpy as jnp
        import numpy as np
        D_MODEL = 128
        D_STATE = 16
        D_CONV = 4
        EXPAND = 2
        D_INNER = EXPAND * D_MODEL
        DT_RANK = D_MODEL // 16
        B_, L_ = (2, 128)

        def _selective_scan(u, dt, A, Bm, Cm, D):
            dA = jnp.exp(dt[..., None] * A)
            dBu = (dt * u)[..., None] * Bm[:, :, None, :]

            def step(h, inp):
                dA_t, dBu_t = inp
                h = dA_t * h + dBu_t
                return (h, h)
            h0 = jnp.zeros((u.shape[0], u.shape[2], A.shape[1]), u.dtype)
            _, hs = jax.lax.scan(step, h0, (dA.swapaxes(0, 1), dBu.swapaxes(0, 1)))
            y = jnp.einsum('lbdn,bln->bld', hs, Cm)
            return y + u * D
        key = jax.random.key(seed)
        ks = jax.random.split(key, 8)
        s = 0.02
        A_log = jnp.log(jnp.tile(jnp.arange(1, D_STATE + 1, dtype=jnp.float32)[None, :], (D_INNER, 1)))
        return {'x': jax.random.normal(ks[0], (B_, L_, D_MODEL), jnp.float32), 'ln_g': jnp.ones((D_MODEL,), jnp.float32), 'ln_b': jnp.zeros((D_MODEL,), jnp.float32), 'in_proj_w': jax.random.normal(ks[1], (2 * D_INNER, D_MODEL), jnp.float32) * s, 'conv_w': jax.random.normal(ks[2], (D_INNER, 1, D_CONV), jnp.float32) * s, 'conv_b': jnp.zeros((D_INNER,), jnp.float32), 'x_proj_w': jax.random.normal(ks[3], (DT_RANK + 2 * D_STATE, D_INNER), jnp.float32) * s, 'dt_proj_w': jax.random.normal(ks[4], (D_INNER, DT_RANK), jnp.float32) * s, 'dt_proj_b': jnp.full((D_INNER,), -4.6, jnp.float32), 'A_log': A_log, 'D': jnp.ones((D_INNER,), jnp.float32), 'out_proj_w': jax.random.normal(ks[5], (D_MODEL, D_INNER), jnp.float32) * s, 'glu_w': jax.random.normal(ks[6], (2 * D_MODEL, D_MODEL), jnp.float32) * s, 'glu_b': jnp.zeros((2 * D_MODEL,), jnp.float32)}
    _L0_attn_in = _L0_attn_setup()

    def _L0_ffn_setup():
        import jax, jax.numpy as jnp
        import numpy as np
        DMODEL = 128
        N_EXPERTS = 32
        EXPERT_SIZE = 64
        N_HEADS = 4
        WEIGHT_SCALE = 1.0
        key = jax.random.key(seed)
        k0, k1, k2, k3 = jax.random.split(key, 4)
        x = jax.random.normal(k0, (2, 256, DMODEL), dtype=jnp.float32)
        expert_sel = jax.random.normal(k1, (N_EXPERTS, DMODEL), dtype=jnp.float32) * DMODEL ** (-0.5)
        keys = jax.random.normal(k2, (N_EXPERTS, DMODEL, EXPERT_SIZE), dtype=jnp.float32) * DMODEL ** (-0.5)
        values = jax.random.normal(k3, (N_EXPERTS, EXPERT_SIZE, DMODEL), dtype=jnp.float32) * (N_EXPERTS * EXPERT_SIZE) ** (-0.5)
        return {'x': x, 'expert_sel': expert_sel, 'keys': keys, 'values': values}
    _L0_ffn_in = _L0_ffn_setup()
    _d = {'L0_attn_x': _L0_attn_in['x'], 'L0_attn_ln_g': _L0_attn_in['ln_g'], 'L0_attn_ln_b': _L0_attn_in['ln_b'], 'L0_attn_in_proj_w': _L0_attn_in['in_proj_w'], 'L0_attn_conv_w': _L0_attn_in['conv_w'], 'L0_attn_conv_b': _L0_attn_in['conv_b'], 'L0_attn_x_proj_w': _L0_attn_in['x_proj_w'], 'L0_attn_dt_proj_w': _L0_attn_in['dt_proj_w'], 'L0_attn_dt_proj_b': _L0_attn_in['dt_proj_b'], 'L0_attn_A_log': _L0_attn_in['A_log'], 'L0_attn_D': _L0_attn_in['D'], 'L0_attn_out_proj_w': _L0_attn_in['out_proj_w'], 'L0_attn_glu_w': _L0_attn_in['glu_w'], 'L0_attn_glu_b': _L0_attn_in['glu_b'], 'L0_ffn_expert_sel': _L0_ffn_in['expert_sel'], 'L0_ffn_keys': _L0_ffn_in['keys'], 'L0_ffn_values': _L0_ffn_in['values']}
    _x0 = _d['L0_attn_x']
    _d['L0_attn_x'] = jax.random.normal(jax.random.fold_in(jax.random.key(seed), 1), (16, 512, 128), dtype=_x0.dtype)
    del _x0
    return _d

def reference(L0_attn_x, L0_attn_ln_g, L0_attn_ln_b, L0_attn_in_proj_w, L0_attn_conv_w, L0_attn_conv_b, L0_attn_x_proj_w, L0_attn_dt_proj_w, L0_attn_dt_proj_b, L0_attn_A_log, L0_attn_D, L0_attn_out_proj_w, L0_attn_glu_w, L0_attn_glu_b, L0_ffn_expert_sel, L0_ffn_keys, L0_ffn_values):

    def _L0_attn_ref(x, ln_g, ln_b, in_proj_w, conv_w, conv_b, x_proj_w, dt_proj_w, dt_proj_b, A_log, D, out_proj_w, glu_w, glu_b):
        import jax, jax.numpy as jnp
        import numpy as np
        D_MODEL = 128
        D_STATE = 16
        D_CONV = 4
        EXPAND = 2
        D_INNER = EXPAND * D_MODEL
        DT_RANK = D_MODEL // 16
        B_, L_ = (2, 128)

        def _selective_scan(u, dt, A, Bm, Cm, D):
            dA = jnp.exp(dt[..., None] * A)
            dBu = (dt * u)[..., None] * Bm[:, :, None, :]

            def step(h, inp):
                dA_t, dBu_t = inp
                h = dA_t * h + dBu_t
                return (h, h)
            h0 = jnp.zeros((u.shape[0], u.shape[2], A.shape[1]), u.dtype)
            _, hs = jax.lax.scan(step, h0, (dA.swapaxes(0, 1), dBu.swapaxes(0, 1)))
            y = jnp.einsum('lbdn,bln->bld', hs, Cm)
            return y + u * D
        skip = x
        mu = x.mean(-1, keepdims=True)
        var = x.var(-1, keepdims=True)
        xn = (x - mu) * jax.lax.rsqrt(var + 1e-05) * ln_g + ln_b
        xz = xn @ in_proj_w.T
        xp, z = (xz[..., :D_INNER], xz[..., D_INNER:])
        xc = jax.lax.conv_general_dilated(xp.transpose(0, 2, 1), conv_w, (1,), [(D_CONV - 1, 0)], dimension_numbers=('NCH', 'OIH', 'NCH'), feature_group_count=D_INNER)
        xc = jax.nn.silu((xc + conv_b[:, None]).transpose(0, 2, 1))
        x_dbl = xc @ x_proj_w.T
        dt = x_dbl[..., :DT_RANK]
        Bm = x_dbl[..., DT_RANK:DT_RANK + D_STATE]
        Cm = x_dbl[..., DT_RANK + D_STATE:]
        dt = jax.nn.softplus(dt @ dt_proj_w.T + dt_proj_b)
        A = -jnp.exp(A_log)
        y = _selective_scan(xc, dt, A, Bm, Cm, D)
        y = y * jax.nn.silu(z)
        m = y @ out_proj_w.T
        m = jax.nn.gelu(m, approximate=False)
        g = m @ glu_w.T + glu_b
        m = g[..., :D_MODEL] * jax.nn.sigmoid(g[..., D_MODEL:])
        return m + skip

    def _L0_ffn_ref(x, expert_sel, keys, values):
        import jax, jax.numpy as jnp
        import numpy as np
        DMODEL = 128
        N_EXPERTS = 32
        EXPERT_SIZE = 64
        N_HEADS = 4
        WEIGHT_SCALE = 1.0
        B, S, D = x.shape
        xt = x.reshape(-1, D)
        N = xt.shape[0]
        sel_logits = jnp.einsum('nd,ed->ne', xt, expert_sel)
        gates = jax.nn.sigmoid(sel_logits)
        sel_val, sel_idx = jax.lax.top_k(gates, N_HEADS)
        gate_full = jnp.zeros_like(gates).at[jnp.arange(N)[:, None], sel_idx].set(sel_val)
        scores = jax.nn.relu(jnp.einsum('nd,edf->nef', xt, keys))
        scores = scores * gate_full[:, :, None]
        out = jnp.einsum('nef,efv->nv', scores, values)
        return out.reshape(B, S, -1)
    x = L0_attn_x
    xn = _layernorm(x, axis=-1)
    x = x + _L0_attn_ref(xn, L0_attn_ln_g, L0_attn_ln_b, L0_attn_in_proj_w, L0_attn_conv_w, L0_attn_conv_b, L0_attn_x_proj_w, L0_attn_dt_proj_w, L0_attn_dt_proj_b, L0_attn_A_log, L0_attn_D, L0_attn_out_proj_w, L0_attn_glu_w, L0_attn_glu_b) + _L0_ffn_ref(xn, L0_ffn_expert_sel, L0_ffn_keys, L0_ffn_values)
    return x

_drawn_inputs = setup_inputs


def setup_inputs(seed=0):
    import zlib

    import numpy as np

    out = dict(_drawn_inputs(seed))
    spreads = {'L0_attn_ln_g': (1.0, 0.6),
     'L0_attn_ln_b': (0.0, 0.8),
     'L0_attn_conv_b': (0.0, 0.8),
     'L0_attn_dt_proj_b': (-4.599999904632568, 0.6),
     'L0_attn_D': (1.0, 0.6),
     'L0_attn_glu_b': (0.0, 0.987)}
    factors = {'L0_attn_in_proj_w': 8.0,
     'L0_attn_conv_w': 8.0,
     'L0_attn_x_proj_w': 8.0,
     'L0_attn_dt_proj_w': 8.0,
     'L0_attn_A_log': 8.0,
     'L0_attn_out_proj_w': 8.0,
     'L0_attn_glu_w': 8.0,
     'L0_ffn_expert_sel': 5.208,
     'L0_ffn_keys': 5.867,
     'L0_ffn_values': 4.911}
    for name, (base, spread) in spreads.items():
        noise = np.random.default_rng([zlib.crc32(name.encode()), seed]).standard_normal(out[name].shape)
        drawn = base * np.exp(spread * noise) if base else spread * noise
        out[name] = jnp.asarray(drawn.astype(out[name].dtype))
    for name, factor in factors.items():
        out[name] = (out[name] * factor).astype(out[name].dtype)
    return out
```

```python
import concourse.bass as bass
from concourse import mybir
from contextlib import ExitStack
from collections import namedtuple

P = 128
Seq = namedtuple("Seq", "b par half")


def after(s):
    return Seq(s.b + 1, 1 - s.par, s.half + s.par)


def before(s):
    return Seq(s.b - 1, 1 - s.par, s.half - (1 - s.par))


def mamba_moe(nc, x, ln_g, ln_b, in_w, conv_w, conv_b, xp_w, dtp_w, dtp_b, a_log, d_skip, out_w,
              glu_w, glu_b, sel_w, keys, values, out):
    fp32, bf16 = mybir.dt.float32, mybir.dt.bfloat16
    ALU, ACT = mybir.AluOpType, mybir.ActivationFunctionType
    B, L, D = x.shape
    H = in_w.shape[0] // 2 // P
    TAPS = conv_w.shape[2]
    N = a_log.shape[1]
    R = dtp_w.shape[1]
    E, _, F = keys.shape
    T = L // P
    TOP = 4
    LOADS = 16
    EPS = 1e-5
    BC = 2 * N
    STACK = 3 * BC
    PAIRS = E * F // P
    assert PAIRS == N and STACK == 3 * E and T * P == L and L == 512

    MISC = {1: ["yT0", "yT1"], 2: ["m"], 3: ["xnT", "xn2T"], 4: ["g1", "g0"], 5: ["conv0"],
            6: ["fin", "conv1"], 7: ["z0"], 8: ["xdbl"], 9: ["gT"], 10: ["z1"], 11: ["dt0", "dt1"]}
    BACK = {"yT0", "yT1", "m", "g1", "g0", "fin"}
    FRONT = [j for i in sorted(MISC) for j in MISC[i] if j not in BACK]
    ORDER = [j for i in range(N) for j in [f"C{i}", f"G{i}"] + MISC.get(i, [])]
    FIRST = [j for j in ORDER if j not in BACK]
    LAST = [j for j in ORDER if j not in FRONT]
    TAIL = [j for j in ORDER if j in BACK]
    assert len(FRONT) % 2 == len(ORDER) % 2 == 0

    def ring(stage, now, job):
        if stage == "pro":
            n = FRONT.index(job)
        elif stage == "first":
            n = len(FRONT) + FIRST.index(job)
        else:
            at = {"body": ORDER, "last": LAST, "epi": TAIL}[stage].index(job)
            lead = (len(FRONT) + len(FIRST)) // 2 + at // 2 + 1
            if stage == "epi":
                return at % 2, lead + (len(ORDER) * (B - 2) + len(LAST)) // 2
            return at % 2, (now.b - 1) * (len(ORDER) // 2) + lead
        return n % 2, n // 2 + 1

    LOGIT_STEP = 5

    def score_job(stage, now, job):
        if stage == "pro":
            return 1
        if job == "logits":
            return now.b * (N + 1) + LOGIT_STEP + 3
        return now.b * (N + 1) + job + 2 + (job > LOGIT_STEP and stage != "last")

    ctx = ExitStack()
    with ctx:
        def sb(name, shape, dt=fp32):
            return ctx.enter_context(nc.sbuf_tensor(name, shape, dt))

        def sem(name):
            return ctx.enter_context(nc.semaphore(name))

        win = sb("win", [P, 2 * H, D])
        xpw = sb("xpw", [R + BC, H * P])
        dtw = sb("dtw", [P, H, R])
        ow = sb("ow", [P, H * P])
        gw = sb("gw", [P, 2, D])
        selw = sb("selw", [E, D])
        key_sb = sb("key_sb", [P, E, F])
        val_sb = sb("val_sb", [P, PAIRS, D])
        alog = sb("alog", [P, H, N])
        lng = sb("lng", [P, 1])
        lnb = sb("lnb", [P, 1])
        cw = sb("cw", [P, H, TAPS])
        cb = sb("cb", [P, H])
        dtb = sb("dtb", [P, H])
        dsk = sb("dsk", [P, H])
        glb = sb("glb", [P, 2])
        ones = sb("ones", [P, P])
        ident = sb("ident", [P, P])
        ident16 = sb("ident16", [P, P], bf16)
        win_tap = sb("win_tap", [P, TAPS, H, D])
        dtw_pad = sb("dtw_pad", [P, H, STACK + R])
        conv_t = sb("conv_t", [P, TAPS, H, P])
        wz_t = sb("wz_t", [P, H * P])
        ow_t = sb("ow_t", [P, H, D])
        gw_t = sb("gw_t", [P, 2, D])
        dtw_t = sb("dtw_t", [P, H, P])
        xp_t = sb("xp_t", [P, H, STACK + R])
        sel_t = sb("sel_t", [P, E])
        diag_d = sb("diag_d", [P, H, P])
        a_neg = sb("a_neg", [P, H, N])
        cb_half = sb("cb_half", [P, H])
        glb_half = sb("glb_half", [P, 1])
        pick = sb("pick", [P, BC])
        pick_bc = sb("pick_bc", [STACK, BC, P], bf16)
        pick_g = sb("pick_g", [STACK, E, F], bf16)
        xt = sb("xt", [P, 2, T, D])
        stats = sb("stats", [P, T, 6])
        mv = sb("mv", [P, T, 2])
        rstd = sb("rstd", [P, 2, T])
        vtmp = sb("vtmp", [P, T])
        minus_half = sb("minus_half", [P, T])
        eps = sb("eps", [P, T])
        xn = sb("xn", [P, T, D])
        xn2 = sb("xn2", [P, T, D])
        xres = sb("xres", [P, 2, T, D])
        xnT = sb("xnT", [P, 2, L])
        xn2T = sb("xn2T", [P, TAPS - 1 + L])
        cpre = sb("cpre", [P, H, L])
        cth = sb("cth", [P, H, L])
        xc = sb("xc", [P, H, L])
        zth = sb("zth", [P, T, H * P])
        sz = sb("sz", [P, 2, T, H * P])
        lth = sb("lth", [P, T, E])
        gates = sb("gates", [P, T, E + TOP])
        gates_left = sb("gates_left", [P, T, E + TOP])
        top8 = sb("top8", [P, T, 8])
        gtop = sb("gtop", [P, T, E])
        grest = sb("grest", [P, T, E])
        g3 = sb("g3", [P, T, STACK], bf16)
        gT = sb("gT", [STACK, 2, L], bf16)
        bc3 = sb("bc3", [STACK, 2, L], bf16)
        bcrest = sb("bcrest", [2 * BC, L])
        dtr = sb("dtr", [P, L])
        dabs = sb("dabs", [P, H, L])
        drelu = sb("drelu", [P, H, L])
        dexp = sb("dexp", [P, H, L])
        dln = sb("dln", [P, H, L])
        drest = sb("drest", [P, H, L])
        dt = sb("dt", [P, 2, H, L])
        dtu = sb("dtu", [P, 2, H, L])
        dA = sb("dA", [P, 2, H, L])
        h = sb("h", [P, 2, H, L])
        hC = sb("hC", [P, 2, H, L])
        Cs = sb("Cs", [P, 2, L])
        Gs = sb("Gs", [P, 2, L])
        hg = sb("hg", [P, 2, L])
        moe_s = sb("moe_s", [P, L])
        yz = sb("yz", [P, T, H * P])
        yT = sb("yT", [P, H, L])
        mg = sb("mg", [P, L])
        th2 = sb("th2", [P, L])
        sg2 = sb("sg2", [P, L])
        m2 = sb("m2", [P, L])
        outb = sb("outb", [P, 2, T, D])

        ps = ctx.enter_context(nc.psum_tensor("ps", [P, 8, 512], fp32))
        RING, SCORE, MOE, YACC = 2, 4, 5, 6

        w_in, ident_ready, halves_ready = sem("w_in"), sem("ident_ready"), sem("halves_ready")
        pads_ready, prep_pe, prep_copied = sem("pads_ready"), sem("prep_pe"), sem("prep_copied")
        a_exp_ready, small_ready = sem("a_exp_ready"), sem("small_ready")
        x_in = [sem("x_in0"), sem("x_in1")]
        stored = [sem("stored0"), sem("stored1")]
        filled = [sem("filled0"), sem("filled1")]
        emptied = [sem("emptied0"), sem("emptied1")]
        score_filled, score_read = sem("score_filled"), sem("score_read")
        b_ready, dbu_ready, da_ready = sem("b_ready"), sem("dbu_ready"), sem("da_ready")
        scan_done, hc_ready, y_done, moe_done = sem("scan_done"), sem("hc_ready"), sem("y_done"), sem("moe_done")
        mv_ready, rstd_ready, xn_ready, xres_ready = sem("mv_ready"), sem("rstd_ready"), sem("xn_ready"), sem("xres_ready")
        g3_ready, xc_ready, hi_ready, dtr_ready = sem("g3_ready"), sem("xc_ready"), sem("hi_ready"), sem("dtr_ready")
        zth_ready, bc_ready, ln_ready = sem("zth_ready"), sem("bc_ready"), sem("ln_ready")
        dt_ready, dtu_ready = sem("dt_ready"), sem("dtu_ready")
        moe_s_ready, yz_ready, m2_ready = sem("moe_s_ready"), sem("yz_ready"), sem("m2_ready")

        x_v = x.rearrange("b (j p) d -> b p j d", p=P)
        out_v = out.rearrange("b (j p) d -> b p j d", p=P)
        first_seq, last_seq = Seq(0, 0, 0), Seq(B - 1, (B - 1) % 2, (B - 1) // 2)

        def walk(eng, body):
            body("first", first_seq)
            with eng.Fori(0, (B - 2) // 2) as pair:
                body("body", Seq(2 * pair + 1, 1, pair))
                body("body", Seq(2 * pair + 2, 0, pair + 1))
            body("last", last_seq)

        def wait_filled(eng, stage, now, job):
            k, n = ring(stage, now, job)
            eng.wait_ge(filled[k], n)
            return k

        def wait_emptied(eng, stage, now, job):
            k, n = ring(stage, now, job)
            eng.wait_ge(emptied[k], n)

        block = ctx.enter_context(nc.Block())

        @block.sync
        def _(sp):
            def load_x(s):
                sp.dma_start(xt[:, s.par], x_v[s.b]).then_inc(x_in[s.par], 16)

            def store_out(stage, now, s):
                wait_emptied(sp, stage, now, "fin")
                sp.dma_start(out_v[s.b], outb[:, s.par]).then_inc(stored[s.par], 16)

            load_x(first_seq)
            loads = [
                (win, in_w.rearrange("(r p) d -> p r d", p=P)),
                (cw, conv_w.rearrange("(h p) o k -> p h (o k)", p=P)),
                (xpw, xp_w), (dtw, dtp_w.rearrange("(h p) r -> p h r", p=P)),
                (ow, out_w), (gw, glu_w.rearrange("(r p) d -> p r d", p=P)), (selw, sel_w),
                (alog, a_log.rearrange("(h p) n -> p h n", p=P)),
                (lng, ln_g.unsqueeze(1)), (lnb, ln_b.unsqueeze(1)),
                (cb, conv_b.rearrange("(h p) -> p h", p=P)), (dtb, dtp_b.rearrange("(h p) -> p h", p=P)),
                (dsk, d_skip.rearrange("(h p) -> p h", p=P)), (glb, glu_b.rearrange("(h p) -> p h", p=P)),
                (key_sb, keys.rearrange("e d f -> d e f")),
                (val_sb, values.rearrange("(i a) f v -> (a f) i v", a=P // F)),
            ]
            assert len(loads) == LOADS
            with nc.allow_non_contiguous_dma(reason="vectors of 256 elements, loaded once"):
                for to, what in loads:
                    sp.dma_start(to[:], what).then_inc(w_in, 16)

            def body(stage, s):
                if stage == "first":
                    load_x(after(s))
                elif stage == "body":
                    sp.wait_ge(xres_ready, s.b)
                    load_x(after(s))
                if stage != "first":
                    store_out(stage, s, before(s))

            walk(sp, body)
            store_out("epi", None, last_seq)
            sp.wait_ge(stored[0], 16 * (B // 2 + 1))
            sp.wait_ge(stored[1], 16 * (B // 2 + 1))

        @block.gpsimd
        def _(pool):
            nc.gpsimd.memset(ones[:], 1.0)
            nc.gpsimd.memset(minus_half[:], -0.5)
            nc.gpsimd.memset(eps[:], EPS)
            nc.gpsimd.drain()
            nc.gpsimd.affine_select(out=ident[:], in_=ones[:], compare_op=ALU.is_equal, fill=0.0, base=0,
                                    pattern=[[-1, P]], channel_multiplier=1).then_inc(ident_ready, 1)

            def norm_scales(s):
                pool.wait_ge(mv_ready, s.b + 1)
                nc.gpsimd.tensor_tensor(vtmp[:], mv[:, :, 1], eps[:], ALU.add)
                nc.gpsimd.drain()
                nc.gpsimd.tensor_tensor(rstd[:, 0], vtmp[:], minus_half[:], ALU.pow)
                nc.gpsimd.drain()
                nc.gpsimd.tensor_tensor(vtmp[:], mv[:, :, 1], rstd[:, 0], ALU.mult)
                nc.gpsimd.drain()
                nc.gpsimd.tensor_tensor(vtmp[:], vtmp[:], rstd[:, 0], ALU.mult)
                nc.gpsimd.drain()
                nc.gpsimd.tensor_scalar(vtmp[:], vtmp[:], EPS, None, ALU.add)
                nc.gpsimd.drain()
                nc.gpsimd.tensor_tensor(rstd[:, 1], vtmp[:], minus_half[:], ALU.pow).then_inc(rstd_ready, 1)

            def residual(s):
                pool.wait_ge(xn_ready, s.b + 1)
                nc.gpsimd.tensor_tensor(xres[:, s.par], xt[:, s.par], xn[:], ALU.add).then_inc(xres_ready, 1)

            norm_scales(first_seq)
            residual(first_seq)

            def body(stage, s):
                for i in range(N):
                    n = s.b * N + i + 1
                    pool.wait_ge(scan_done, n)
                    wait_emptied(pool, stage, s, f"C{i}")
                    if stage != "first" or i >= 2:
                        pool.wait_ge(y_done, n - 2)
                    c_row = Cs[:, i % 2].unsqueeze(1).broadcast_to([P, H, L])
                    nc.gpsimd.tensor_tensor(hC[:, i % 2], h[:, i % 2], c_row, ALU.mult).then_inc(hc_ready, 1)
                    if stage != "last" and i == 1:
                        norm_scales(after(s))
                    if stage != "last" and i == 7:
                        if stage != "first":
                            wait_emptied(pool, stage, s, "fin")
                        residual(after(s))

            walk(pool, body)

        @block.scalar
        def _(act):
            def to_sbuf(dst, src, scale=1.0):
                return nc.scalar.activation(dst, src, ACT.Copy, scale=scale)

            act.wait_ge(w_in, 16 * LOADS)
            nc.scalar.activation(a_neg[:], alog[:], ACT.Exp).then_inc(a_exp_ready, 1)
            act.wait_ge(prep_pe, 1)
            to_sbuf(conv_t[:, 0:2], ps[:, 0].rearrange("p (k h c) -> p k h c", k=2, h=H))
            act.wait_ge(prep_pe, 2)
            to_sbuf(conv_t[:, 2:4], ps[:, 1].rearrange("p (k h c) -> p k h c", k=2, h=H))
            act.wait_ge(prep_pe, 3)
            to_sbuf(wz_t[:], ps[:, 2, 0:2 * P], scale=0.5)
            to_sbuf(ow_t[:], ps[:, 2, 2 * P:4 * P].rearrange("p (h m) -> p h m", h=H))
            act.wait_ge(prep_pe, 4)
            to_sbuf(gw_t[:], ps[:, 3, 0:2 * P].rearrange("p (h m) -> p h m", h=2))
            to_sbuf(dtw_t[STACK:STACK + R], ps[STACK:STACK + R, 3, 2 * P:4 * P].rearrange("p (h m) -> p h m", h=H))
            act.wait_ge(prep_pe, 5)
            xp_ps = ps[:, 4, 0:H * (R + BC)].rearrange("p (h c) -> p h c", h=H)
            for k in range(3):
                to_sbuf(xp_t[:, :, k * BC:(k + 1) * BC], xp_ps[:, :, R:R + BC])
            to_sbuf(xp_t[:, :, STACK:STACK + R], xp_ps[:, :, 0:R])
            to_sbuf(sel_t[:], ps[:, 4, P:P + E]).then_inc(prep_copied, 1)
            act.wait_ge(small_ready, 1)

            def front_xT(stage, now, s):
                k = wait_filled(act, stage, now, "xnT")
                to_sbuf(xnT[:, s.par], ps[:, RING + k]).then_inc(emptied[k], 1)
                k = wait_filled(act, stage, now, "xn2T")
                nc.scalar.activation(xn2T[:, TAPS - 1:], ps[:, RING + k], ACT.Identity, bias=lnb[:, 0:1],
                                     scale=lng[:, 0:1]).then_inc(emptied[k], 1)

            def front_logits(stage, now):
                act.wait_ge(score_filled, score_job(stage, now, "logits"))
                nc.scalar.activation(lth[:], ps[:, SCORE, 0:T * E].rearrange("p (j e) -> p j e", j=T), ACT.Tanh,
                                     scale=0.5).then_inc(score_read, 1)

            def front_conv(stage, now, hh):
                k = wait_filled(act, stage, now, f"conv{hh}")
                nc.scalar.activation(cpre[:, hh], ps[:, RING + k], ACT.Identity, bias=cb_half[:, hh:hh + 1])
                nc.scalar.activation(cth[:, hh], ps[:, RING + k], ACT.Tanh,
                                     bias=cb_half[:, hh:hh + 1]).then_inc(emptied[k], 1)

            def front_z(stage, now, part):
                k = wait_filled(act, stage, now, f"z{part}")
                nc.scalar.activation(zth[:, 2 * part:2 * part + 2], ps[:, RING + k].rearrange("p (j c) -> p j c", j=2),
                                     ACT.Tanh).then_inc(zth_ready, 1)

            def front_xdbl(stage, now, s):
                k = wait_filled(act, stage, now, "xdbl")
                to_sbuf(bc3[:, s.par], ps[0:STACK, RING + k]).then_inc(hi_ready, 1)
                to_sbuf(dtr[STACK:STACK + R], ps[STACK:STACK + R, RING + k]).then_inc(dtr_ready, 1)

            def front_gT(stage, now, s):
                k = wait_filled(act, stage, now, "gT")
                to_sbuf(gT[:, s.par], ps[0:STACK, RING + k, 0:L // 2].bitcast(bf16)).then_inc(emptied[k], 1)

            def front_dt(stage, now):
                for hh in range(H):
                    k = wait_filled(act, stage, now, f"dt{hh}")
                    nc.scalar.activation(dabs[:, hh], ps[:, RING + k], ACT.Abs, bias=dtb[:, hh:hh + 1])
                    nc.scalar.activation(drelu[:, hh], ps[:, RING + k], ACT.Relu,
                                         bias=dtb[:, hh:hh + 1]).then_inc(emptied[k], 1)
                nc.scalar.drain()
                nc.scalar.activation(dexp[:], dabs[:], ACT.Exp, scale=-1.0)
                nc.scalar.drain()
                nc.scalar.activation(dln[:], dexp[:], ACT.Ln, bias=1.0).then_inc(ln_ready, 1)

            def back_moe(s):
                act.wait_ge(moe_done, (s.b + 1) * N)
                to_sbuf(moe_s[:], ps[:, MOE]).then_inc(moe_s_ready, 1)

            def back_yT(stage, now):
                for hh in range(H):
                    k = wait_filled(act, stage, now, f"yT{hh}")
                    to_sbuf(yT[:, hh], ps[:, RING + k]).then_inc(emptied[k], 1)

            def back_gelu(stage, now):
                k = wait_filled(act, stage, now, "m")
                nc.scalar.activation(mg[:], ps[:, RING + k], ACT.Gelu).then_inc(emptied[k], 1)

            def back_glu(stage, now):
                k = wait_filled(act, stage, now, "g1")
                nc.scalar.activation(th2[:], ps[:, RING + k], ACT.Tanh, bias=glb_half[:, 0:1],
                                     scale=0.5).then_inc(emptied[k], 1)

            front_xT("pro", None, first_seq)
            front_logits("pro", None)
            front_conv("pro", None, 0)
            front_conv("pro", None, 1)
            front_z("pro", None, 0)
            front_xdbl("pro", None, first_seq)
            front_gT("pro", None, first_seq)
            front_z("pro", None, 1)
            front_dt("pro", None)

            def body(stage, s):
                for i in range(N):
                    n = s.b * N + i + 1
                    if i == 0:
                        act.wait_ge(dt_ready, s.b + 1)
                    if stage != "first" or i >= 2:
                        act.wait_ge(scan_done, n - 2)
                    for hh in range(H):
                        last = nc.scalar.activation(dA[:, i % 2, hh, 1:L], dt[:, s.par, hh, 1:L], ACT.Exp,
                                                    scale=a_neg[:, hh, i:i + 1])
                    last.then_inc(da_ready, 1)
                    k = wait_filled(act, stage, s, f"C{i}")
                    if stage != "first" or i >= 2:
                        act.wait_ge(hc_ready, n - 2)
                    to_sbuf(Cs[:, i % 2], ps[:, RING + k]).then_inc(emptied[k], 1)
                    k = wait_filled(act, stage, s, f"G{i}")
                    if stage != "first" or i >= 2:
                        act.wait_ge(score_read, score_job(stage, s, i - 2))
                    to_sbuf(Gs[:, i % 2], ps[:, RING + k]).then_inc(emptied[k], 1)
                    if stage != "first":
                        if i == 0:
                            back_moe(before(s))
                        if i == 1:
                            back_yT(stage, s)
                        if i == 2:
                            back_gelu(stage, s)
                        if i == 4:
                            back_glu(stage, s)
                    if stage != "last":
                        if i == 3:
                            front_xT(stage, s, after(s))
                        if i == 5:
                            front_logits(stage, s)
                            front_conv(stage, s, 0)
                        if i == 6:
                            front_conv(stage, s, 1)
                        if i == 7:
                            front_z(stage, s, 0)
                        if i == 8:
                            front_xdbl(stage, s, after(s))
                        if i == 9:
                            front_gT(stage, s, after(s))
                        if i == 10:
                            front_z(stage, s, 1)
                        if i == 11:
                            front_dt(stage, s)

            walk(act, body)
            back_moe(last_seq)
            back_yT("epi", None)
            back_gelu("epi", None)
            back_glu("epi", None)

        @block.vector
        def _(dve):
            nc.vector.memset(dA[:], 0.0)
            nc.vector.memset(xn2T[:, 0:TAPS - 1], 0.0)
            nc.vector.memset(gates[:, :, E:], 2.0)
            nc.vector.memset(dtw_pad[:], 0.0)
            for k in range(2):
                nc.vector.memset(outb[:, k], 0.0).then_inc(stored[k], 16)
            dve.wait_ge(w_in, 16 * LOADS)
            dve.wait_ge(ident_ready, 1)
            for k in range(TAPS):
                for hh in range(H):
                    last = nc.vector.tensor_scalar(win_tap[:, k, hh], win[:, hh], cw[:, hh, k:k + 1], 0.5,
                                                   ALU.mult, ALU.mult)
            last.then_inc(halves_ready, 1)
            nc.vector.drain()
            nc.vector.tensor_copy(dtw_pad[:, :, STACK:], dtw[:]).then_inc(pads_ready, 1)
            nc.vector.tensor_copy(ident16[:], ident[:])
            nc.vector.tensor_tensor(pick[:], ident[:, 0:BC], ident[:, BC:2 * BC], ALU.add)
            nc.vector.drain()
            nc.vector.tensor_tensor(pick[:], pick[:], ident[:, 2 * BC:3 * BC], ALU.add)
            nc.vector.drain()
            nc.vector.tensor_copy(pick_bc[:], pick[0:STACK].unsqueeze(2).broadcast_to([STACK, BC, P]))
            nc.vector.tensor_copy(pick_g[:], pick[0:STACK].unsqueeze(2).broadcast_to([STACK, E, F]))
            for hh in range(H):
                nc.vector.tensor_scalar(diag_d[:, hh], ident[:], dsk[:, hh:hh + 1], None, ALU.mult)
            nc.vector.tensor_scalar(cb_half[:], cb[:], 0.5, None, ALU.mult)
            nc.vector.tensor_scalar(glb_half[:], glb[:, 1:2], 0.5, None, ALU.mult)
            dve.wait_ge(a_exp_ready, 1)
            nc.vector.tensor_scalar(a_neg[:], a_neg[:], -1.0, None, ALU.mult).then_inc(small_ready, 1)

            def front_stats(s):
                dve.wait_ge(x_in[s.par], 16 * (s.half + 1))
                for j in range(T):
                    nc.vector.bn_stats(stats[:, j], xt[:, s.par, j])
                nc.vector.drain()
                for j in range(T):
                    last = nc.vector.bn_aggr(mv[:, j], stats[:, j])
                last.then_inc(mv_ready, 1)

            def front_xn(s):
                dve.wait_ge(rstd_ready, s.b + 1)
                for j in range(T):
                    nc.vector.tensor_scalar(xn[:, j], xt[:, s.par, j], mv[:, j, 0:1], rstd[:, 0, j:j + 1],
                                            ALU.subtract, ALU.mult)
                nc.vector.drain()
                for j in range(T):
                    last = nc.vector.tensor_scalar(xn2[:, j], xn[:, j], rstd[:, 1, j:j + 1], None, ALU.mult)
                last.then_inc(xn_ready, 1)

            def front_gates(stage, now):
                dve.wait_ge(score_read, score_job(stage, now, "logits"))
                nc.vector.tensor_scalar(gates[:, :, 0:E], lth[:], 0.5, 0.5, ALU.mult, ALU.add)
                nc.vector.drain()
                for j in range(T):
                    nc.vector.max(top8[:, j], gates[:, j, 0:E])
                nc.vector.drain()
                nc.vector.memset(top8[:, :, TOP:], 2.0)
                nc.vector.drain()
                for j in range(T):
                    nc.vector.match_replace(out=gates_left[:, j], in_to_replace=top8[:, j], in_values=gates[:, j],
                                            imm_value=0.0)
                nc.vector.drain()
                nc.vector.tensor_tensor(gtop[:], gates[:, :, 0:E], gates_left[:, :, 0:E], ALU.subtract)
                nc.vector.drain()
                nc.vector.tensor_copy(g3[:, :, 2 * E:], gtop[:])
                nc.vector.drain()
                nc.vector.tensor_tensor(grest[:], gtop[:], g3[:, :, 2 * E:], ALU.subtract)
                nc.vector.drain()
                nc.vector.tensor_copy(g3[:, :, E:2 * E], grest[:])
                nc.vector.drain()
                nc.vector.tensor_tensor(g3[:, :, 0:E], grest[:], g3[:, :, E:2 * E], ALU.subtract).then_inc(g3_ready, 1)

            def front_xc(stage, now, s):
                wait_emptied(dve, stage, now, "conv0")
                wait_emptied(dve, stage, now, "conv1")
                nc.vector.scalar_tensor_tensor(xc[:], cth[:], 1.0, cpre[:], ALU.add, ALU.mult).then_inc(xc_ready, 1)

            def front_sz(stage, now, s, part):
                dve.wait_ge(zth_ready, 2 * s.b + part + 1)
                k, _ = ring(stage, now, f"z{part}")
                nc.vector.scalar_tensor_tensor(sz[:, s.par, 2 * part:2 * part + 2], zth[:, 2 * part:2 * part + 2], 1.0,
                                               ps[:, RING + k].rearrange("p (j c) -> p j c", j=2),
                                               ALU.add, ALU.mult).then_inc(emptied[k], 1)

            def front_bc(stage, now, s):
                dve.wait_ge(hi_ready, s.b + 1)
                dve.wait_ge(dtr_ready, s.b + 1)
                k, _ = ring(stage, now, "xdbl")
                nc.vector.tensor_tensor(bcrest[:], ps[0:2 * BC, RING + k], bc3[0:2 * BC, s.par],
                                        ALU.subtract).then_inc(emptied[k], 1)
                nc.vector.drain()
                nc.vector.tensor_copy(bc3[0:2 * BC, s.par], bcrest[:])
                nc.vector.drain()
                nc.vector.tensor_tensor(bc3[0:BC, s.par], bcrest[0:BC], bc3[0:BC, s.par],
                                        ALU.subtract).then_inc(bc_ready, 1)

            def front_dt(s):
                dve.wait_ge(ln_ready, s.b + 1)
                nc.vector.tensor_scalar(drest[:], dexp[:], 1.0, 1.0, ALU.add, ALU.subtract)
                nc.vector.tensor_tensor(dln[:], dln[:], drelu[:], ALU.add)
                nc.vector.drain()
                nc.vector.tensor_tensor(drest[:], dexp[:], drest[:], ALU.subtract)
                nc.vector.drain()
                nc.vector.tensor_tensor(dt[:, s.par], dln[:], drest[:], ALU.add).then_inc(dt_ready, 1)
                nc.vector.drain()
                nc.vector.tensor_tensor(dtu[:, s.par], dt[:, s.par], xc[:], ALU.mult).then_inc(dtu_ready, 1)

            def back_yz(s):
                dve.wait_ge(y_done, (s.b + 1) * N)
                nc.vector.tensor_tensor(yz[:], ps[:, YACC:YACC + 2].rearrange("p k (j c) -> p (k j) c", j=2), sz[:, s.par],
                                        ALU.mult).then_inc(yz_ready, 1)

            def back_glu(stage, now):
                wait_emptied(dve, stage, now, "g1")
                nc.vector.tensor_scalar(sg2[:], th2[:], 0.5, 0.5, ALU.mult, ALU.add)
                nc.vector.drain()
                k = wait_filled(dve, stage, now, "g0")
                nc.vector.scalar_tensor_tensor(m2[:], ps[:, RING + k], glb[:, 0:1], sg2[:], ALU.add,
                                               ALU.mult).then_inc(emptied[k], 1)

            def back_out(stage, now, s):
                k = wait_filled(dve, stage, now, "fin")
                dve.wait_ge(xres_ready, s.b + 1)
                dve.wait_ge(stored[s.par], 16 * (s.half + 1))
                nc.vector.tensor_tensor(outb[:, s.par], ps[:, RING + k].rearrange("p (j d) -> p j d", j=T),
                                        xres[:, s.par], ALU.add).then_inc(emptied[k], 1)

            front_stats(first_seq)
            front_xn(first_seq)
            front_gates("pro", None)
            front_xc("pro", None, first_seq)
            front_sz("pro", None, first_seq, 0)
            front_bc("pro", None, first_seq)
            front_sz("pro", None, first_seq, 1)
            front_dt(first_seq)

            def body(stage, s):
                for i in range(N):
                    n = s.b * N + i + 1
                    dve.wait_ge(b_ready, n)
                    if i == 0:
                        dve.wait_ge(dtu_ready, s.b + 1)
                    b_row = ps[:, 1].unsqueeze(1).broadcast_to([P, H, L])
                    nc.vector.tensor_tensor(ps[:, 0:2], dtu[:, s.par], b_row, ALU.mult).then_inc(dbu_ready, 1)
                    dve.wait_ge(da_ready, n)
                    if stage != "first" or i >= 2:
                        dve.wait_ge(hc_ready, n - 2)
                    dve.wait_ge(dbu_ready, n)
                    nc.vector.tensor_tensor_scan(h[:, i % 2].rearrange("p h t -> p (h t)"),
                                                 dA[:, i % 2].rearrange("p h t -> p (h t)"),
                                                 ps[:, 0:2].rearrange("p h t -> p (h t)"), 0.0, ALU.mult,
                                                 ALU.add).then_inc(scan_done, 1)
                    dve.wait_ge(score_filled, score_job(stage, s, i))
                    wait_emptied(dve, stage, s, f"G{i}")
                    if stage != "first" or i >= 2:
                        dve.wait_ge(moe_done, n - 2)
                    nc.vector.scalar_tensor_tensor(hg[:, i % 2], ps[:, SCORE], 0.0, Gs[:, i % 2], ALU.max,
                                                   ALU.mult).then_inc(score_read, 1)
                    if stage != "first":
                        if i == 0:
                            back_yz(before(s))
                        if i == 4:
                            back_glu(stage, s)
                        if i == 6:
                            back_out(stage, s, before(s))
                    if stage != "last":
                        if i == 1:
                            front_stats(after(s))
                        if i == 2:
                            front_xn(after(s))
                        if i == 6:
                            front_gates(stage, s)
                        if i == 7:
                            front_xc(stage, s, after(s))
                            front_sz(stage, s, after(s), 0)
                        if i == 8:
                            front_bc(stage, s, after(s))
                        if i == 10:
                            front_sz(stage, s, after(s), 1)
                        if i == 13:
                            front_dt(after(s))

            walk(dve, body)
            back_yz(last_seq)
            back_glu("epi", None)
            back_out("epi", None, last_seq)

        @block.tensor
        def _(pe):
            def turn(dst, src, start=True, **more):
                return nc.tensor.matmul(dst, src, ident[0:src.shape[0], 0:src.shape[0]], is_transpose=True,
                                        start=start, stop=True, **more)

            pe.wait_ge(ident_ready, 1)
            pe.wait_ge(w_in, 16 * LOADS)
            pe.wait_ge(halves_ready, 1)
            for k in range(TAPS):
                for hh in range(H):
                    at = (k % 2 * H + hh) * P
                    last = turn(ps[:, k // 2, at:at + P], win_tap[:, k, hh])
                if k % 2:
                    last.then_inc(prep_pe, 1)
            for hh in range(H):
                turn(ps[:, 2, hh * P:(hh + 1) * P], win[:, H + hh])
                last = turn(ps[:, 2, (H + hh) * P:(H + hh + 1) * P], ow[:, hh * P:(hh + 1) * P])
            last.then_inc(prep_pe, 1)
            pe.wait_ge(pads_ready, 1)
            for hh in range(H):
                turn(ps[:, 3, hh * P:(hh + 1) * P], gw[:, hh])
                last = turn(ps[0:STACK + R, 3, (H + hh) * P:(H + hh + 1) * P], dtw_pad[:, hh])
            last.then_inc(prep_pe, 1)
            for hh in range(H):
                turn(ps[:, 4, hh * (R + BC):(hh + 1) * (R + BC)], xpw[:, hh * P:(hh + 1) * P])
            turn(ps[:, 4, P:P + E], selw[:]).then_inc(prep_pe, 1)
            pe.wait_ge(prep_copied, 1)
            pe.wait_ge(small_ready, 1)

            def take(stage, now, job):
                k, n = ring(stage, now, job)
                if stage != "pro" or n > 1:
                    pe.wait_ge(emptied[k], n - 1)
                return k

            def front_xT(stage, now, s):
                pe.wait_ge(xn_ready, s.b + 1)
                for job, src in (("xnT", xn), ("xn2T", xn2)):
                    k = take(stage, now, job)
                    for j in range(T):
                        last = turn(ps[:, RING + k, j * P:(j + 1) * P], src[:, j])
                    last.then_inc(filled[k], 1)

            def front_logits(stage, now, s):
                wait_emptied(pe, stage, now, "xnT")
                if stage != "pro":
                    pe.wait_ge(score_read, score_job(stage, now, "logits") - 1)
                for j in range(T):
                    last = nc.tensor.matmul(ps[:, SCORE, j * E:(j + 1) * E], xnT[:, s.par, j * P:(j + 1) * P], sel_t[:],
                                            start=True, stop=True)
                last.then_inc(score_filled, 1)

            def front_conv(stage, now, hh):
                if hh == 0:
                    wait_emptied(pe, stage, now, "xn2T")
                k = take(stage, now, f"conv{hh}")
                for tap in range(TAPS):
                    last = nc.tensor.matmul(ps[:, RING + k], conv_t[:, tap, hh], xn2T[:, tap:tap + L],
                                            start=(tap == 0), stop=(tap == TAPS - 1))
                last.then_inc(filled[k], 1)

            def front_z(stage, now, part):
                k = take(stage, now, f"z{part}")
                for j in range(2):
                    at = TAPS - 1 + (2 * part + j) * P
                    last = nc.tensor.matmul(ps[:, RING + k, j * H * P:(j + 1) * H * P], xn2T[:, at:at + P], wz_t[:],
                                            start=True, stop=True)
                last.then_inc(filled[k], 1)

            def front_xdbl(stage, now, s):
                pe.wait_ge(xc_ready, s.b + 1)
                k = take(stage, now, "xdbl")
                for hh in range(H):
                    last = nc.tensor.matmul(ps[0:STACK + R, RING + k], xp_t[:, hh], xc[:, hh], start=(hh == 0),
                                            stop=(hh == H - 1))
                last.then_inc(filled[k], 1)

            def front_gT(stage, now, s):
                pe.wait_ge(g3_ready, s.b + 1)
                k = take(stage, now, "gT")
                for j in range(T):
                    last = nc.tensor.matmul(ps[0:STACK, RING + k, j * P // 2:(j + 1) * P // 2].bitcast(bf16), g3[:, j],
                                            ident16[:], is_transpose=True, start=True, stop=True)
                last.then_inc(filled[k], 1)

            def front_dt(stage, now, s):
                pe.wait_ge(dtr_ready, s.b + 1)
                for hh in range(H):
                    k = take(stage, now, f"dt{hh}")
                    nc.tensor.matmul(ps[:, RING + k], dtw_t[STACK:STACK + R, hh], dtr[STACK:STACK + R],
                                     start=True, stop=True).then_inc(filled[k], 1)
                wait_emptied(pe, stage, now, "gT")

            def back_yT(stage, now, s):
                pe.wait_ge(yz_ready, s.b + 1)
                for hh in range(H):
                    k = take(stage, now, f"yT{hh}")
                    for j in range(T):
                        last = turn(ps[:, RING + k, j * P:(j + 1) * P], yz[:, j, hh * P:(hh + 1) * P])
                    last.then_inc(filled[k], 1)

            def back_m(stage, now):
                wait_emptied(pe, stage, now, "yT0")
                wait_emptied(pe, stage, now, "yT1")
                k = take(stage, now, "m")
                for hh in range(H):
                    last = nc.tensor.matmul(ps[:, RING + k], ow_t[:, hh], yT[:, hh], start=(hh == 0), stop=(hh == H - 1))
                last.then_inc(filled[k], 1)

            def back_glu(stage, now):
                wait_emptied(pe, stage, now, "m")
                for r in (1, 0):
                    k = take(stage, now, f"g{r}")
                    nc.tensor.matmul(ps[:, RING + k], gw_t[:, r], mg[:], start=True, stop=True).then_inc(filled[k], 1)

            def back_fin(stage, now, s):
                wait_emptied(pe, stage, now, "g0")
                pe.wait_ge(moe_s_ready, s.b + 1)
                k = take(stage, now, "fin")
                for j in range(T):
                    at = slice(j * P, (j + 1) * P)
                    turn(ps[:, RING + k, at], moe_s[:, at])
                    last = turn(ps[:, RING + k, at], m2[:, at], start=False, skip_group_check=True)
                last.then_inc(filled[k], 1)

            def sum_y(stage, s, i):
                if i == 0:
                    if stage != "first":
                        pe.wait_ge(yz_ready, s.b)
                    for j in range(T):
                        for hh in range(H):
                            nc.tensor.matmul(ps[:, YACC + j // 2, (j % 2 * H + hh) * P:(j % 2 * H + hh + 1) * P],
                                             xc[:, hh, j * P:(j + 1) * P], diag_d[:, hh], start=(j % 2 + hh == 0),
                                             stop=False, skip_group_check=True)
                pe.wait_ge(hc_ready, s.b * N + i + 1)
                for j in range(T):
                    for hh in range(H):
                        last = turn(ps[:, YACC + j // 2, (j % 2 * H + hh) * P:(j % 2 * H + hh + 1) * P],
                                    hC[:, i % 2, hh, j * P:(j + 1) * P], start=False, skip_group_check=True)
                last.then_inc(y_done, 1)

            def sum_moe(stage, s, i, gated):
                if i == 0 and stage != "first":
                    pe.wait_ge(moe_s_ready, s.b)
                pe.wait_ge(score_read, gated)
                nc.tensor.matmul(ps[:, MOE], val_sb[:, i], hg[:, i % 2], start=(i == 0),
                                 stop=(i == N - 1)).then_inc(moe_done, 1)

            front_xT("pro", None, first_seq)
            front_logits("pro", None, first_seq)
            front_conv("pro", None, 0)
            front_conv("pro", None, 1)
            front_z("pro", None, 0)
            front_xdbl("pro", None, first_seq)
            front_gT("pro", None, first_seq)
            front_z("pro", None, 1)
            front_dt("pro", None, first_seq)

            def body(stage, s):
                for i in range(N):
                    n = s.b * N + i + 1
                    if i == 0:
                        pe.wait_ge(bc_ready, s.b + 1)
                    if stage != "first" or i >= 1:
                        pe.wait_ge(scan_done, n - 1)
                    nc.tensor.matmul(ps[:, 1], pick_bc[:, i], bc3[:, s.par], start=True, stop=True).then_inc(b_ready, 1)
                    k = take(stage, s, f"C{i}")
                    nc.tensor.matmul(ps[:, RING + k], pick_bc[:, N + i], bc3[:, s.par], start=True,
                                     stop=True).then_inc(filled[k], 1)
                    pe.wait_ge(score_read, score_job(stage, s, i) - 1)
                    nc.tensor.matmul(ps[:, SCORE], key_sb[:, 2 * i:2 * i + 2].rearrange("p e f -> p (e f)"),
                                     xnT[:, s.par], start=True, stop=True).then_inc(score_filled, 1)
                    k = take(stage, s, f"G{i}")
                    nc.tensor.matmul(ps[:, RING + k], pick_g[:, 2 * i:2 * i + 2].rearrange("p e f -> p (e f)"),
                                     gT[:, s.par], start=True, stop=True).then_inc(filled[k], 1)
                    if i > 0:
                        sum_y(stage, s, i - 1)
                        sum_moe(stage, s, i - 1, score_job(stage, s, i - 1))
                    elif stage != "first":
                        sum_y(stage, before(s), N - 1)
                        sum_moe(stage, before(s), N - 1, score_job(stage, s, -1))
                    if stage != "first":
                        if i == 1:
                            back_yT(stage, s, before(s))
                        if i == 2:
                            back_m(stage, s)
                        if i == 4:
                            back_glu(stage, s)
                        if i == 6:
                            back_fin(stage, s, before(s))
                    if stage != "last":
                        if i == 3:
                            front_xT(stage, s, after(s))
                        if i == LOGIT_STEP:
                            front_logits(stage, s, after(s))
                            front_conv(stage, s, 0)
                        if i == 6:
                            front_conv(stage, s, 1)
                        if i == 7:
                            front_z(stage, s, 0)
                        if i == 8:
                            front_xdbl(stage, s, after(s))
                        if i == 9:
                            front_gT(stage, s, after(s))
                        if i == 10:
                            front_z(stage, s, 1)
                        if i == 11:
                            front_dt(stage, s, after(s))

            walk(pe, body)
            sum_y("last", last_seq, N - 1)
            sum_moe("last", last_seq, N - 1, score_job("last", last_seq, N - 1))
            back_yT("epi", None, last_seq)
            back_m("epi", None)
            back_glu("epi", None)
            back_fin("epi", None, last_seq)


_INS = ["L0_attn_x", "L0_attn_ln_g", "L0_attn_ln_b", "L0_attn_in_proj_w", "L0_attn_conv_w", "L0_attn_conv_b",
        "L0_attn_x_proj_w", "L0_attn_dt_proj_w", "L0_attn_dt_proj_b", "L0_attn_A_log", "L0_attn_D",
        "L0_attn_out_proj_w", "L0_attn_glu_w", "L0_attn_glu_b", "L0_ffn_expert_sel", "L0_ffn_keys", "L0_ffn_values"]


def kernel(**inputs):
    import numpy as _np
    import concourse.bacc as _bacc
    from concourse import mybir as _mybir
    from concourse.bass_utils import run_bass_kernel_spmd as _run

    nc = _bacc.Bacc("TRN2", target_bir_lowering=False, num_devices=1)
    arrays, args = {}, []
    for name in _INS:
        a = _np.ascontiguousarray(inputs[name])
        arrays[f"in_{name}_dram"] = a
        args.append(nc.dram_tensor(f"in_{name}_dram", a.shape, _mybir.dt.from_np(a.dtype), kind="ExternalInput").ap())
    shape = inputs["L0_attn_x"].shape
    args.append(nc.dram_tensor("out_dram", shape, _mybir.dt.float32, kind="ExternalOutput").ap())
    mamba_moe(nc, *args)
    r = _run(nc, [arrays], core_ids=[0])
    return r.results[0]["out_dram"]
```

```python
import concourse.bass as bass
from concourse import mybir
from contextlib import ExitStack
from collections import namedtuple

P = 128
Seq = namedtuple("Seq", "b par half")


def after(s):
    return Seq(s.b + 1, 1 - s.par, s.half + s.par)


def before(s):
    return Seq(s.b - 1, 1 - s.par, s.half - (1 - s.par))


def mamba_moe(nc, x, ln_g, ln_b, in_w, conv_w, conv_b, xp_w, dtp_w, dtp_b, a_log, d_skip, out_w,
              glu_w, glu_b, sel_w, keys, values, out):
    fp32, f32r, bf16 = mybir.dt.float32, mybir.dt.float32r, mybir.dt.bfloat16
    ALU, ACT = mybir.AluOpType, mybir.ActivationFunctionType
    B, L, D = x.shape
    H = in_w.shape[0] // 2 // P
    TAPS = conv_w.shape[2]
    N = a_log.shape[1]
    R = dtp_w.shape[1]
    E, _, F = keys.shape
    T = L // P
    TOP = 4
    GATE_LAG, Y_LAG, MOE_LAG = 1, 2, 2
    LOADS = 16
    EPS = 1e-5
    BC = 2 * N
    STACK = 3 * BC
    PAIRS = E * F // P
    assert PAIRS == N and STACK == 3 * E and T * P == L and L == 512

    AT = {"yT": 3, "m": 4, "glu": 10, "fin": 12, "xT": 2, "logits": 3, "conv0": 4, "conv1": 4, "xdbl": 7, "dt": 8, "z0": 11, "z1": 12, "gT": 13}
    AT_ACT = {"moe": 1, "exp": 10, "ln": 12}
    AT_DVE = {"yz": 1, "glu": 11, "fin": 12, "stats": 0, "xn": 2, "xT": 2, "gates": 9, "xc": 5, "bc": 8, "bc_low": 11, "round": 11, "z0": 11, "z1": 13, "dt": 14}
    AT_POOL = {"norm": 0, "rest": 11, "sum": 12, "residual": 15}
    JOBS = {"yT": ["yT0", "yT1"], "m": ["m"], "glu": ["g1", "g0"], "fin": ["fin0", "fin1"], "xT": ["xnT", "xn2T"],
            "dt": ["dt0", "dt1"]}
    MISC = {i: [job for piece in AT if AT[piece] == i for job in JOBS.get(piece, [piece])] for i in range(N)}
    BACK = {"yT0", "yT1", "m", "g1", "g0", "fin0", "fin1"}
    FRONT = ["xnT", "xn2T", "logits", "conv0", "conv1", "xdbl", "dt0", "dt1", "z0", "z1", "gT"]
    ORDER = [j for i in range(N) for j in [f"C{i}", f"S{i}", f"G{i}"] + MISC[i]]
    FIRST = [j for j in ORDER if j not in BACK]
    LAST = [j for j in ORDER if j not in FRONT]
    TAIL = [j for j in ORDER if j in BACK]
    LOOPED = len(FRONT) + len(FIRST)
    assert len(ORDER) % 2 == LOOPED % 2 == 0

    def ring(stage, now, job, ago=0):
        table = {"pro": FRONT, "first": FIRST, "body": ORDER, "last": LAST, "epi": TAIL}[stage]
        at = ORDER.index(job) - len(ORDER) if ago else table.index(job)
        if stage == "body" or stage == "last":
            return at % 2, (now.b - 1) * (len(ORDER) // 2) + LOOPED // 2 + at // 2 + 1
        at += {"pro": 0, "first": len(FRONT), "epi": LOOPED + len(ORDER) * (B - 2) + len(LAST)}[stage]
        return at % 2, at // 2 + 1

    ctx = ExitStack()
    with ctx:
        def sb(name, shape, dt=fp32):
            return ctx.enter_context(nc.sbuf_tensor(name, shape, dt))

        def sem(name):
            return ctx.enter_context(nc.semaphore(name))

        hC = sb("hC", [P, 4, H, L])
        win = hC[:, 2, 0].rearrange("p (r d) -> p r d", d=D)
        key_sb = hC[:, 0:2].rearrange("p a h (e f) -> p (a h e) f", f=F)
        xpw = sb("xpw", [R + BC, H * P])
        dtw = sb("dtw", [P, H, R])
        ow = hC[:, 2, 1, 0:H * P]
        gw = hC[:, 2, 1, H * P:].rearrange("p (r d) -> p r d", d=D)
        selw = sb("selw", [E, D])
        val_sb = sb("val_sb", [P, PAIRS, D])
        alog = sb("alog", [P, H, N])
        lng = sb("lng", [P, 1])
        lnb = sb("lnb", [P, 1])
        cw = sb("cw", [P, H, TAPS])
        cb = sb("cb", [P, H])
        dtb = sb("dtb", [P, H])
        dsk = sb("dsk", [P, H])
        glb = sb("glb", [P, 2])
        ones = sb("ones", [P, P])
        ident = sb("ident", [P, P])
        ident16 = sb("ident16", [P, P], bf16)
        win_tap = hC[:, 3].rearrange("p h (k d) -> p (h k) d", d=D)
        dtw_pad = sb("dtw_pad", [P, H, STACK + R])
        conv_t = sb("conv_t", [P, 2, TAPS, H, P], f32r)
        wz_t = sb("wz_t", [P, 2, H * P], f32r)
        key_t = sb("key_t", [P, 2, E, F], f32r)
        sel_t = sb("sel_t", [P, 2, E], f32r)
        ow_t = sb("ow_t", [P, H, D])
        gw_t = sb("gw_t", [P, 2, D])
        dtw_t = sb("dtw_t", [P, H, P])
        xp_t = sb("xp_t", [P, H, STACK + R])
        diag_d = sb("diag_d", [P, H, P])
        a_neg = sb("a_neg", [P, H, N])
        cb_half = sb("cb_half", [P, H])
        glb_half = sb("glb_half", [P, 1])
        pick = sb("pick", [P, BC])
        pick_bc = sb("pick_bc", [STACK, BC, P], bf16)
        pick_g = sb("pick_g", [STACK, E, F], bf16)
        xt = sb("xt", [P, 2, T, D])
        stats = sb("stats", [P, T, 6])
        mv = sb("mv", [P, T, 2])
        rstd = sb("rstd", [P, 2, T])
        vtmp = sb("vtmp", [P, T])
        minus_half = sb("minus_half", [P, T])
        eps = sb("eps", [P, T])
        xn = sb("xn", [P, T, D])
        xn2 = sb("xn2", [P, T, D])
        xres = sb("xres", [P, 2, T, D])
        xnT = sb("xnT", [P, 2, 2, L], f32r)
        xn2T = sb("xn2T", [P, 2, TAPS - 1 + L], f32r)
        cpre = drelu = sb("conv_then_relu", [P, H, L])
        cth = dln = sb("tanh_then_log", [P, H, L])
        xc = sb("xc", [P, H, L])
        zth = sb("tanh_z_then_yT", [P, T, H * P])
        sz = sb("sz", [P, 2, T, H * P])
        lth = sb("lth", [P, T, E])
        gates = sb("gates", [P, T, E + TOP])
        gates_left = sb("gates_left", [P, T, E + TOP])
        top8 = sb("top8", [P, T, 8])
        gtop = sb("gtop", [P, T, E])
        grest = sb("grest", [P, T, E])
        g3 = sb("g3", [P, T, STACK], bf16)
        gT = sb("gT", [STACK, 2, L], bf16)
        bc3 = sb("bc3", [STACK, 2, L], bf16)
        bcrest = sb("bcrest", [2 * BC, L])
        dtr = sb("dtr", [P, L])
        dexp = sb("dexp", [P, H, L])
        drest = sb("rest_then_yz", [P, H, L])
        dt = sb("dt", [P, 2, H, L])
        dtu = sb("dtu", [P, 2, H, L])
        dA = sb("dA", [P, 2, H, L])
        h = sb("h", [P, 2, H, L])
        relu_s = sb("relu_s", [P, 4, L])
        Cs = sb("Cs", [P, 2, L])
        Gs = sb("Gs", [P, 4, L])
        hg = sb("hg", [P, 2, L])
        moe_s = sb("moe_s", [P, L])
        yz = drest[:].rearrange("p h l -> p (h l)").rearrange("p (t c) -> p t c", t=T)
        yT = zth[:].rearrange("p t (h c) -> p (t h c)", h=H).rearrange("p (h l) -> p h l", h=H)
        mg = sb("mg", [P, L])
        th2 = xn2T_full = sb("th2", [P, L])
        m2 = sb("m2", [P, L])
        outb = sb("outb", [P, 2, T, D])

        ps = ctx.enter_context(nc.psum_tensor("ps", [P, 8, 512], fp32))
        RING, MOE, YACC = 3, 5, 6

        split_hi, split_lo = sem("split_hi"), sem("split_lo")
        w_in, ident_ready, halves_ready = sem("w_in"), sem("ident_ready"), sem("halves_ready")
        pads_ready, prep_pe = sem("pads_ready"), sem("prep_pe")
        a_exp_ready, small_ready = sem("a_exp_ready"), sem("small_ready")
        x_in = [sem("x_in0"), sem("x_in1")]
        stored = [sem("stored0"), sem("stored1")]
        filled = [sem("filled0"), sem("filled1")]
        emptied = [sem("emptied0"), sem("emptied1")]
        b_ready, dbu_ready, da_ready = sem("b_ready"), sem("dbu_ready"), sem("da_ready")
        hg_ready = sem("hg_ready")
        scan_done, hc_ready, y_done, moe_done = sem("scan_done"), sem("hc_ready"), sem("y_done"), sem("moe_done")
        exp_ready = sem("exp_ready")
        rounded_ready, rest_ready, sum_ready = sem("rounded_ready"), sem("rest_ready"), sem("sum_ready")
        mv_ready, rstd_ready, xn_ready, xres_ready = sem("mv_ready"), sem("rstd_ready"), sem("xn_ready"), sem("xres_ready")
        g3_ready, xc_ready, hi_ready, dtr_ready = sem("g3_ready"), sem("xc_ready"), sem("hi_ready"), sem("dtr_ready")
        xnT_hi, xn2T_low = sem("xnT_hi"), sem("xn2T_low")
        zth_ready, bc_ready, ln_ready = sem("zth_ready"), sem("bc_ready"), sem("ln_ready")
        dt_ready, dtu_ready = sem("dt_ready"), sem("dtu_ready")
        moe_s_ready, yz_ready, m2_ready = sem("moe_s_ready"), sem("yz_ready"), sem("m2_ready")

        x_v = x.rearrange("b (j p) d -> b p j d", p=P)
        out_v = out.rearrange("b (j p) d -> b p j d", p=P)
        first_seq, last_seq = Seq(0, 0, 0), Seq(B - 1, (B - 1) % 2, (B - 1) // 2)

        def walk(eng, body):
            body("first", first_seq)
            with eng.Fori(0, (B - 2) // 2) as pair:
                body("body", Seq(2 * pair + 1, 1, pair))
                body("body", Seq(2 * pair + 2, 0, pair + 1))
            body("last", last_seq)

        def wait_filled(eng, stage, now, job):
            k, n = ring(stage, now, job)
            eng.wait_ge(filled[k], n)
            return k

        def wait_emptied(eng, stage, now, job, ago=0):
            k, n = ring(stage, now, job, ago)
            eng.wait_ge(emptied[k], n)

        block = ctx.enter_context(nc.Block())

        @block.sync
        def _(sp):
            def load_x(s):
                sp.dma_start(xt[:, s.par], x_v[s.b]).then_inc(x_in[s.par], 16)

            def store_out(stage, now, s):
                wait_emptied(sp, stage, now, "fin1")
                sp.dma_start(out_v[s.b], outb[:, s.par]).then_inc(stored[s.par], 16)

            load_x(first_seq)
            loads = [
                (win, in_w.rearrange("(r p) d -> p r d", p=P)),
                (cw, conv_w.rearrange("(h p) o k -> p h (o k)", p=P)),
                (xpw, xp_w), (dtw, dtp_w.rearrange("(h p) r -> p h r", p=P)),
                (ow, out_w), (gw, glu_w.rearrange("(r p) d -> p r d", p=P)), (selw, sel_w),
                (alog, a_log.rearrange("(h p) n -> p h n", p=P)),
                (lng, ln_g.unsqueeze(1)), (lnb, ln_b.unsqueeze(1)),
                (cb, conv_b.rearrange("(h p) -> p h", p=P)), (dtb, dtp_b.rearrange("(h p) -> p h", p=P)),
                (dsk, d_skip.rearrange("(h p) -> p h", p=P)), (glb, glu_b.rearrange("(h p) -> p h", p=P)),
                (key_sb, keys.rearrange("e d f -> d e f")),
                (val_sb, values.rearrange("(i a) f v -> (a f) i v", a=P // F)),
            ]
            assert len(loads) == LOADS
            with nc.allow_non_contiguous_dma(reason="vectors of 256 elements, loaded once"):
                for to, what in loads:
                    sp.dma_start(to[:], what).then_inc(w_in, 16)

            def body(stage, s):
                if stage == "first":
                    load_x(after(s))
                elif stage == "body":
                    sp.wait_ge(xres_ready, s.b)
                    load_x(after(s))
                if stage != "first":
                    store_out(stage, s, before(s))

            walk(sp, body)
            store_out("epi", None, last_seq)
            sp.wait_ge(stored[0], 16 * (B // 2 + 1))
            sp.wait_ge(stored[1], 16 * (B // 2 + 1))

        @block.gpsimd
        def _(pool):
            nc.gpsimd.memset(ones[:], 1.0)
            nc.gpsimd.memset(minus_half[:], -0.5)
            nc.gpsimd.memset(eps[:], EPS)
            nc.gpsimd.drain()
            nc.gpsimd.affine_select(out=ident[:], in_=ones[:], compare_op=ALU.is_equal, fill=0.0, base=0,
                                    pattern=[[-1, P]], channel_multiplier=1).then_inc(ident_ready, 1)

            def norm_scales(s):
                pool.wait_ge(mv_ready, s.b + 1)
                nc.gpsimd.tensor_tensor(vtmp[:], mv[:, :, 1], eps[:], ALU.add)
                nc.gpsimd.drain()
                nc.gpsimd.tensor_tensor(rstd[:, 0], vtmp[:], minus_half[:], ALU.pow)
                nc.gpsimd.drain()
                nc.gpsimd.tensor_tensor(vtmp[:], mv[:, :, 1], rstd[:, 0], ALU.mult)
                nc.gpsimd.drain()
                nc.gpsimd.tensor_tensor(vtmp[:], vtmp[:], rstd[:, 0], ALU.mult)
                nc.gpsimd.drain()
                nc.gpsimd.tensor_scalar(vtmp[:], vtmp[:], EPS, None, ALU.add)
                nc.gpsimd.drain()
                nc.gpsimd.tensor_tensor(rstd[:, 1], vtmp[:], minus_half[:], ALU.pow).then_inc(rstd_ready, 1)

            def residual(s):
                pool.wait_ge(xn_ready, s.b + 1)
                nc.gpsimd.tensor_tensor(xres[:, s.par], xt[:, s.par], xn[:], ALU.add).then_inc(xres_ready, 1)

            def softplus_rest(s):
                pool.wait_ge(rounded_ready, s.b + 1)
                nc.gpsimd.tensor_tensor(drest[:], dexp[:], drest[:], ALU.subtract).then_inc(rest_ready, 1)

            def softplus_sum(s):
                pool.wait_ge(ln_ready, s.b + 1)
                nc.gpsimd.tensor_tensor(dln[:], dln[:], drelu[:], ALU.add).then_inc(sum_ready, 1)

            def gate(stage, now, i, n, ago=0, reused=True):
                wait_emptied(pool, stage, now, f"S{i}", ago)
                wait_emptied(pool, stage, now, f"G{i}", ago)
                if reused:
                    pool.wait_ge(moe_done, n - 2)
                nc.gpsimd.tensor_tensor(hg[:, i % 2], relu_s[:, i % 4], Gs[:, i % 4], ALU.mult).then_inc(hg_ready, 1)

            norm_scales(first_seq)
            residual(first_seq)
            softplus_rest(first_seq)
            softplus_sum(first_seq)

            def body(stage, s):
                for i in range(N):
                    n = s.b * N + i + 1
                    if i >= GATE_LAG:
                        gate(stage, s, i - GATE_LAG, n - GATE_LAG, reused=stage != "first" or i >= GATE_LAG + 2)
                    elif stage != "first":
                        gate(stage, s, N + i - GATE_LAG, n - GATE_LAG, ago=1)
                    pool.wait_ge(scan_done, n)
                    wait_emptied(pool, stage, s, f"C{i}")
                    if stage != "first" or i >= 4:
                        pool.wait_ge(y_done, n - 4)
                    c_row = Cs[:, i % 2].unsqueeze(1).broadcast_to([P, H, L])
                    nc.gpsimd.tensor_tensor(hC[:, i % 4], h[:, i % 2], c_row, ALU.mult).then_inc(hc_ready, 1)
                    if stage != "last":
                        if i == AT_POOL["norm"]:
                            norm_scales(after(s))
                        if i == AT_POOL["rest"]:
                            softplus_rest(after(s))
                        if i == AT_POOL["sum"]:
                            softplus_sum(after(s))
                        if i == AT_POOL["residual"]:
                            if stage != "first":
                                wait_emptied(pool, stage, s, "fin1")
                            residual(after(s))

            walk(pool, body)
            for i in range(N - GATE_LAG, N):
                gate("last", last_seq, i, (B - 1) * N + i + 1)

        @block.scalar
        def _(act):
            def to_sbuf(dst, src, scale=1.0):
                return nc.scalar.activation(dst, src, ACT.Copy, scale=scale)

            act.wait_ge(w_in, 16 * LOADS)
            nc.scalar.activation(a_neg[:], alog[:], ACT.Exp).then_inc(a_exp_ready, 1)
            act.wait_ge(prep_pe, 1)
            to_sbuf(conv_t[:, 0, 0:2], ps[:, 0].rearrange("p (k h c) -> p k h c", k=2, h=H))
            act.wait_ge(prep_pe, 2)
            to_sbuf(conv_t[:, 0, 2:4], ps[:, 1].rearrange("p (k h c) -> p k h c", k=2, h=H))
            act.wait_ge(prep_pe, 3)
            to_sbuf(wz_t[:, 0], ps[:, 2, 0:2 * P], scale=0.5)
            to_sbuf(ow_t[:], ps[:, 2, 2 * P:4 * P].rearrange("p (h m) -> p h m", h=H))
            act.wait_ge(prep_pe, 4)
            to_sbuf(gw_t[:], ps[:, 3, 0:2 * P].rearrange("p (h m) -> p h m", h=2))
            to_sbuf(dtw_t[STACK:STACK + R], ps[STACK:STACK + R, 3, 2 * P:4 * P].rearrange("p (h m) -> p h m", h=H))
            act.wait_ge(prep_pe, 5)
            xp_ps = ps[:, 4, 0:H * (R + BC)].rearrange("p (h c) -> p h c", h=H)
            for k in range(3):
                to_sbuf(xp_t[:, :, k * BC:(k + 1) * BC], xp_ps[:, :, R:R + BC])
            to_sbuf(xp_t[:, :, STACK:STACK + R], xp_ps[:, :, 0:R])
            to_sbuf(sel_t[:, 0], ps[:, 4, P:P + E]).then_inc(split_hi, 1)
            act.wait_ge(small_ready, 1)

            def front_xT(stage, now, s):
                k = wait_filled(act, stage, now, "xnT")
                to_sbuf(xnT[:, s.par, 0], ps[:, RING + k]).then_inc(xnT_hi, 1)
                k = wait_filled(act, stage, now, "xn2T")
                nc.scalar.activation(xn2T_full[:], ps[:, RING + k], ACT.Identity, bias=lnb[:, 0:1],
                                     scale=lng[:, 0:1])
                nc.scalar.activation(xn2T[:, 0, TAPS - 1:], ps[:, RING + k], ACT.Identity, bias=lnb[:, 0:1],
                                     scale=lng[:, 0:1]).then_inc(emptied[k], 1)

            def front_logits(stage, now):
                k = wait_filled(act, stage, now, "logits")
                nc.scalar.activation(lth[:], ps[:, RING + k, 0:T * E].rearrange("p (j e) -> p j e", j=T), ACT.Tanh,
                                     scale=0.5).then_inc(emptied[k], 1)

            def front_conv(stage, now, hh):
                k = wait_filled(act, stage, now, f"conv{hh}")
                nc.scalar.activation(cpre[:, hh], ps[:, RING + k], ACT.Identity, bias=cb_half[:, hh:hh + 1])
                nc.scalar.activation(cth[:, hh], ps[:, RING + k], ACT.Tanh,
                                     bias=cb_half[:, hh:hh + 1]).then_inc(emptied[k], 1)

            def front_z(stage, now, part):
                k = wait_filled(act, stage, now, f"z{part}")
                nc.scalar.activation(zth[:, 2 * part:2 * part + 2], ps[:, RING + k].rearrange("p (j c) -> p j c", j=2),
                                     ACT.Tanh).then_inc(zth_ready, 1)

            def front_xdbl(stage, now, s):
                k = wait_filled(act, stage, now, "xdbl")
                to_sbuf(bc3[:, s.par], ps[0:STACK, RING + k]).then_inc(hi_ready, 1)
                to_sbuf(dtr[STACK:STACK + R], ps[STACK:STACK + R, RING + k]).then_inc(dtr_ready, 1)

            def front_gT(stage, now, s):
                k = wait_filled(act, stage, now, "gT")
                to_sbuf(gT[:, s.par], ps[0:STACK, RING + k, 0:L // 2].bitcast(bf16)).then_inc(emptied[k], 1)

            def front_dt(stage, now):
                for hh in range(H):
                    k = wait_filled(act, stage, now, f"dt{hh}")
                    nc.scalar.activation(dexp[:, hh], ps[:, RING + k], ACT.Abs, bias=dtb[:, hh:hh + 1])
                    nc.scalar.activation(drelu[:, hh], ps[:, RING + k], ACT.Relu,
                                         bias=dtb[:, hh:hh + 1]).then_inc(emptied[k], 1)

            def front_exp(s):
                nc.scalar.drain()
                nc.scalar.activation(dexp[:], dexp[:], ACT.Exp, scale=-1.0).then_inc(exp_ready, 1)

            def front_ln(s):
                act.wait_ge(exp_ready, s.b + 1)
                nc.scalar.activation(dln[:], dexp[:], ACT.Ln, bias=1.0).then_inc(ln_ready, 1)

            def back_moe(s):
                act.wait_ge(moe_done, (s.b + 1) * N)
                to_sbuf(moe_s[:], ps[:, MOE]).then_inc(moe_s_ready, 1)

            def back_yT(stage, now):
                for hh in range(H):
                    k = wait_filled(act, stage, now, f"yT{hh}")
                    to_sbuf(yT[:, hh], ps[:, RING + k]).then_inc(emptied[k], 1)

            def back_gelu(stage, now):
                k = wait_filled(act, stage, now, "m")
                nc.scalar.activation(mg[:], ps[:, RING + k], ACT.Gelu).then_inc(emptied[k], 1)

            def back_glu(stage, now):
                k = wait_filled(act, stage, now, "g1")
                nc.scalar.activation(th2[:], ps[:, RING + k], ACT.Tanh, bias=glb_half[:, 0:1],
                                     scale=0.5).then_inc(emptied[k], 1)

            front_xT("pro", None, first_seq)
            front_logits("pro", None)
            front_conv("pro", None, 0)
            front_conv("pro", None, 1)
            front_xdbl("pro", None, first_seq)
            front_dt("pro", None)
            front_exp(first_seq)
            front_ln(first_seq)
            front_z("pro", None, 0)
            front_z("pro", None, 1)
            front_gT("pro", None, first_seq)

            def decay(s, i, n, reused=True):
                if i == 0:
                    act.wait_ge(dt_ready, s.b + 1)
                if reused:
                    act.wait_ge(scan_done, n - 2)
                for hh in range(H):
                    last = nc.scalar.activation(dA[:, i % 2, hh, 1:L], dt[:, s.par, hh, 1:L], ACT.Exp,
                                                scale=a_neg[:, hh, i:i + 1])
                last.then_inc(da_ready, 1)

            decay(first_seq, 0, 1, reused=False)

            def body(stage, s):
                for i in range(N):
                    n = s.b * N + i + 1
                    k = wait_filled(act, stage, s, f"C{i}")
                    if stage != "first" or i >= 2:
                        act.wait_ge(hc_ready, n - 2)
                    to_sbuf(Cs[:, i % 2], ps[:, RING + k]).then_inc(emptied[k], 1)
                    if i < N - 1:
                        decay(s, i + 1, n + 1, reused=stage != "first" or i >= 1)
                    elif stage != "last":
                        decay(after(s), 0, n + 1)
                    k = wait_filled(act, stage, s, f"S{i}")
                    if stage != "first" or i >= 4:
                        act.wait_ge(hg_ready, n - 4)
                    nc.scalar.activation(relu_s[:, i % 4], ps[:, RING + k], ACT.Relu).then_inc(emptied[k], 1)
                    k = wait_filled(act, stage, s, f"G{i}")
                    to_sbuf(Gs[:, i % 4], ps[:, RING + k]).then_inc(emptied[k], 1)
                    if stage != "first":
                        if i == AT_ACT["moe"]:
                            back_moe(before(s))
                        if i == AT["yT"]:
                            back_yT(stage, s)
                        if i == AT["m"]:
                            back_gelu(stage, s)
                        if i == AT["glu"]:
                            back_glu(stage, s)
                    if stage != "last":
                        if i == AT["xT"]:
                            front_xT(stage, s, after(s))
                        if i == AT["logits"]:
                            front_logits(stage, s)
                        for hh in range(H):
                            if i == AT[f"conv{hh}"]:
                                front_conv(stage, s, hh)
                        if i == AT["xdbl"]:
                            front_xdbl(stage, s, after(s))
                        if i == AT["dt"]:
                            front_dt(stage, s)
                        if i == AT_ACT["exp"]:
                            front_exp(after(s))
                        if i == AT_ACT["ln"]:
                            front_ln(after(s))
                        for part in range(2):
                            if i == AT[f"z{part}"]:
                                front_z(stage, s, part)
                        if i == AT["gT"]:
                            front_gT(stage, s, after(s))

            walk(act, body)
            back_moe(last_seq)
            back_yT("epi", None)
            back_gelu("epi", None)
            back_glu("epi", None)

        @block.vector
        def _(dve):
            nc.vector.memset(dA[:], 0.0)
            nc.vector.memset(xn2T[:, :, 0:TAPS - 1].bitcast(fp32), 0.0)
            nc.vector.memset(gates[:, :, E:], 2.0)
            nc.vector.memset(dtw_pad[:], 0.0)
            for k in range(2):
                nc.vector.memset(outb[:, k], 0.0).then_inc(stored[k], 16)
            dve.wait_ge(w_in, 16 * LOADS)
            dve.wait_ge(ident_ready, 1)
            for k in range(TAPS):
                for hh in range(H):
                    last = nc.vector.tensor_scalar(win_tap[:, k * H + hh], win[:, hh], cw[:, hh, k:k + 1], 0.5,
                                                   ALU.mult, ALU.mult)
            last.then_inc(halves_ready, 1)
            nc.vector.drain()
            nc.vector.tensor_copy(dtw_pad[:, :, STACK:], dtw[:]).then_inc(pads_ready, 1)
            nc.vector.tensor_copy(ident16[:], ident[:])
            nc.vector.tensor_tensor(pick[:], ident[:, 0:BC], ident[:, BC:2 * BC], ALU.add)
            nc.vector.drain()
            nc.vector.tensor_tensor(pick[:], pick[:], ident[:, 2 * BC:3 * BC], ALU.add)
            nc.vector.drain()
            nc.vector.tensor_copy(pick_bc[:], pick[0:STACK].unsqueeze(2).broadcast_to([STACK, BC, P]))
            nc.vector.tensor_copy(pick_g[:], pick[0:STACK].unsqueeze(2).broadcast_to([STACK, E, F]))
            for hh in range(H):
                nc.vector.tensor_scalar(diag_d[:, hh], ident[:], dsk[:, hh:hh + 1], None, ALU.mult)
            nc.vector.tensor_scalar(cb_half[:], cb[:], 0.5, None, ALU.mult)
            nc.vector.tensor_scalar(glb_half[:], glb[:, 1:2], 0.5, None, ALU.mult)
            dve.wait_ge(a_exp_ready, 1)
            nc.vector.tensor_scalar(a_neg[:], a_neg[:], -1.0, None, ALU.mult).then_inc(small_ready, 1)
            nc.vector.tensor_copy(key_t[:, 0], key_sb[:])
            nc.vector.drain()
            nc.vector.tensor_tensor(key_t[:, 1], key_sb[:], key_t[:, 0], ALU.subtract)
            dve.wait_ge(split_hi, 1)
            nc.vector.tensor_tensor(conv_t[:, 1].rearrange("p k h c -> p (k h c)"),
                                    ps[:, 0:2].rearrange("p b c -> p (b c)"),
                                    conv_t[:, 0].rearrange("p k h c -> p (k h c)"), ALU.subtract)
            nc.vector.scalar_tensor_tensor(wz_t[:, 1], ps[:, 2, 0:2 * P], 0.5, wz_t[:, 0], ALU.mult, ALU.subtract)
            nc.vector.tensor_tensor(sel_t[:, 1], ps[:, 4, P:P + E], sel_t[:, 0], ALU.subtract).then_inc(split_lo, 1)

            def front_stats(s):
                dve.wait_ge(x_in[s.par], 16 * (s.half + 1))
                for j in range(T):
                    nc.vector.bn_stats(stats[:, j], xt[:, s.par, j])
                nc.vector.drain()
                for j in range(T):
                    last = nc.vector.bn_aggr(mv[:, j], stats[:, j])
                last.then_inc(mv_ready, 1)

            def front_xn(s):
                dve.wait_ge(rstd_ready, s.b + 1)
                for j in range(T):
                    nc.vector.tensor_scalar(xn[:, j], xt[:, s.par, j], mv[:, j, 0:1], rstd[:, 0, j:j + 1],
                                            ALU.subtract, ALU.mult)
                nc.vector.drain()
                for j in range(T):
                    last = nc.vector.tensor_scalar(xn2[:, j], xn[:, j], rstd[:, 1, j:j + 1], None, ALU.mult)
                last.then_inc(xn_ready, 1)

            def front_xT_low(stage, now, s):
                dve.wait_ge(xnT_hi, s.b + 1)
                k, _ = ring(stage, now, "xnT")
                nc.vector.tensor_tensor(xnT[:, s.par, 1], ps[:, RING + k], xnT[:, s.par, 0],
                                        ALU.subtract).then_inc(emptied[k], 1)
                wait_emptied(dve, stage, now, "xn2T")
                nc.vector.tensor_tensor(xn2T[:, 1, TAPS - 1:], xn2T_full[:], xn2T[:, 0, TAPS - 1:],
                                        ALU.subtract).then_inc(xn2T_low, 1)

            def front_gates(stage, now):
                wait_emptied(dve, stage, now, "logits")
                nc.vector.tensor_scalar(gates[:, :, 0:E], lth[:], 0.5, 0.5, ALU.mult, ALU.add)
                nc.vector.drain()
                for j in range(T):
                    nc.vector.max(top8[:, j], gates[:, j, 0:E])
                nc.vector.drain()
                nc.vector.memset(top8[:, :, TOP:], 2.0)
                nc.vector.drain()
                for j in range(T):
                    nc.vector.match_replace(out=gates_left[:, j], in_to_replace=top8[:, j], in_values=gates[:, j],
                                            imm_value=0.0)
                nc.vector.drain()
                nc.vector.tensor_tensor(gtop[:], gates[:, :, 0:E], gates_left[:, :, 0:E], ALU.subtract)
                nc.vector.drain()
                nc.vector.tensor_copy(g3[:, :, 2 * E:], gtop[:])
                nc.vector.drain()
                nc.vector.tensor_tensor(grest[:], gtop[:], g3[:, :, 2 * E:], ALU.subtract)
                nc.vector.drain()
                nc.vector.tensor_copy(g3[:, :, E:2 * E], grest[:])
                nc.vector.drain()
                nc.vector.tensor_tensor(g3[:, :, 0:E], grest[:], g3[:, :, E:2 * E], ALU.subtract).then_inc(g3_ready, 1)

            def front_xc(stage, now, s):
                wait_emptied(dve, stage, now, "conv0")
                wait_emptied(dve, stage, now, "conv1")
                nc.vector.scalar_tensor_tensor(xc[:], cth[:], 1.0, cpre[:], ALU.add, ALU.mult).then_inc(xc_ready, 1)

            def front_sz(stage, now, s, part):
                dve.wait_ge(zth_ready, 2 * s.b + part + 1)
                k, _ = ring(stage, now, f"z{part}")
                nc.vector.scalar_tensor_tensor(sz[:, s.par, 2 * part:2 * part + 2], zth[:, 2 * part:2 * part + 2], 1.0,
                                               ps[:, RING + k].rearrange("p (j c) -> p j c", j=2),
                                               ALU.add, ALU.mult).then_inc(emptied[k], 1)

            def front_bc(stage, now, s):
                dve.wait_ge(hi_ready, s.b + 1)
                dve.wait_ge(dtr_ready, s.b + 1)
                k, _ = ring(stage, now, "xdbl")
                nc.vector.tensor_tensor(bcrest[:], ps[0:2 * BC, RING + k], bc3[0:2 * BC, s.par],
                                        ALU.subtract).then_inc(emptied[k], 1)

            def front_bc_low(s):
                nc.vector.drain()
                nc.vector.tensor_copy(bc3[0:2 * BC, s.par], bcrest[:])
                nc.vector.drain()
                nc.vector.tensor_tensor(bc3[0:BC, s.par], bcrest[0:BC], bc3[0:BC, s.par],
                                        ALU.subtract).then_inc(bc_ready, 1)

            def front_round(s):
                dve.wait_ge(exp_ready, s.b + 1)
                nc.vector.tensor_scalar(drest[:], dexp[:], 1.0, 1.0, ALU.add, ALU.subtract).then_inc(rounded_ready, 1)

            def front_dt(s):
                dve.wait_ge(sum_ready, s.b + 1)
                dve.wait_ge(rest_ready, s.b + 1)
                nc.vector.tensor_tensor(dt[:, s.par], dln[:], drest[:], ALU.add).then_inc(dt_ready, 1)
                nc.vector.drain()
                nc.vector.tensor_tensor(dtu[:, s.par], dt[:, s.par], xc[:], ALU.mult).then_inc(dtu_ready, 1)

            def back_yz(s):
                dve.wait_ge(y_done, (s.b + 1) * N)
                nc.vector.tensor_tensor(yz[:], ps[:, YACC:YACC + 2].rearrange("p k (j c) -> p (k j) c", j=2), sz[:, s.par],
                                        ALU.mult).then_inc(yz_ready, 1)

            def back_glu(stage, now):
                wait_emptied(dve, stage, now, "g1")
                nc.vector.tensor_scalar(th2[:], th2[:], 0.5, 0.5, ALU.mult, ALU.add)
                nc.vector.drain()
                k = wait_filled(dve, stage, now, "g0")
                nc.vector.scalar_tensor_tensor(m2[:], ps[:, RING + k], glb[:, 0:1], th2[:], ALU.add,
                                               ALU.mult).then_inc(emptied[k], 1)

            def back_out(stage, now, s):
                dve.wait_ge(xres_ready, s.b + 1)
                dve.wait_ge(stored[s.par], 16 * (s.half + 1))
                for part in range(2):
                    k = wait_filled(dve, stage, now, f"fin{part}")
                    two = slice(2 * part, 2 * part + 2)
                    nc.vector.tensor_tensor(outb[:, s.par, two],
                                            ps[:, RING + k, 0:2 * P].rearrange("p (j d) -> p j d", j=2),
                                            xres[:, s.par, two], ALU.add).then_inc(emptied[k], 1)

            front_stats(first_seq)
            front_xn(first_seq)
            front_xT_low("pro", None, first_seq)
            front_gates("pro", None)
            front_xc("pro", None, first_seq)
            front_bc("pro", None, first_seq)
            front_bc_low(first_seq)
            front_round(first_seq)
            front_dt(first_seq)
            front_sz("pro", None, first_seq, 0)
            front_sz("pro", None, first_seq, 1)

            def body(stage, s):
                for i in range(N):
                    n = s.b * N + i + 1
                    dve.wait_ge(b_ready, n)
                    if i == 0:
                        dve.wait_ge(dtu_ready, s.b + 1)
                    if stage != "first" or i >= 1:
                        dve.wait_ge(scan_done, n - 1)
                    low = 1 - i % 2
                    if low:
                        b_row = ps[:, 2].unsqueeze(1).broadcast_to([P, H, L])
                        nc.vector.tensor_tensor(ps[:, 1:3], dtu[:, s.par], b_row, ALU.mult).then_inc(dbu_ready, 1)
                    else:
                        nc.vector.tensor_tensor(ps[:, 1], dtu[:, s.par, 1], ps[:, 0], ALU.mult)
                        nc.vector.tensor_tensor(ps[:, 0], dtu[:, s.par, 0], ps[:, 0], ALU.mult).then_inc(dbu_ready, 1)
                    dve.wait_ge(da_ready, n)
                    if stage != "first" or i >= 2:
                        dve.wait_ge(hc_ready, n - 2)
                    dve.wait_ge(dbu_ready, n)
                    nc.vector.tensor_tensor_scan(h[:, i % 2].rearrange("p h t -> p (h t)"),
                                                 dA[:, i % 2].rearrange("p h t -> p (h t)"),
                                                 ps[:, low:low + 2].rearrange("p h t -> p (h t)"), 0.0, ALU.mult,
                                                 ALU.add).then_inc(scan_done, 1)
                    if stage != "first":
                        if i == AT_DVE["yz"]:
                            back_yz(before(s))
                        if i == AT_DVE["glu"]:
                            back_glu(stage, s)
                        if i == AT_DVE["fin"]:
                            back_out(stage, s, before(s))
                    if stage != "last":
                        if i == AT_DVE["stats"]:
                            front_stats(after(s))
                        if i == AT_DVE["xn"]:
                            front_xn(after(s))
                        if i == AT_DVE["xT"]:
                            front_xT_low(stage, s, after(s))
                        if i == AT_DVE["gates"]:
                            front_gates(stage, s)
                        if i == AT_DVE["xc"]:
                            front_xc(stage, s, after(s))
                        if i == AT_DVE["bc"]:
                            front_bc(stage, s, after(s))
                        if i == AT_DVE["bc_low"]:
                            front_bc_low(after(s))
                        if i == AT_DVE["round"]:
                            front_round(after(s))
                        for part in range(2):
                            if i == AT_DVE[f"z{part}"]:
                                front_sz(stage, s, after(s), part)
                        if i == AT_DVE["dt"]:
                            front_dt(after(s))

            walk(dve, body)
            back_yz(last_seq)
            back_glu("epi", None)
            back_out("epi", None, last_seq)

        @block.tensor
        def _(pe):
            def turn(dst, src, start=True, **more):
                return nc.tensor.matmul(dst, src, ident[0:src.shape[0], 0:src.shape[0]], is_transpose=True,
                                        start=start, stop=True, **more)

            pe.wait_ge(ident_ready, 1)
            pe.wait_ge(w_in, 16 * LOADS)
            pe.wait_ge(halves_ready, 1)
            for k in range(TAPS):
                for hh in range(H):
                    at = (k % 2 * H + hh) * P
                    last = turn(ps[:, k // 2, at:at + P], win_tap[:, k * H + hh])
                if k % 2:
                    last.then_inc(prep_pe, 1)
            for hh in range(H):
                turn(ps[:, 2, hh * P:(hh + 1) * P], win[:, H + hh])
                last = turn(ps[:, 2, (H + hh) * P:(H + hh + 1) * P], ow[:, hh * P:(hh + 1) * P])
            last.then_inc(prep_pe, 1)
            pe.wait_ge(pads_ready, 1)
            for hh in range(H):
                turn(ps[:, 3, hh * P:(hh + 1) * P], gw[:, hh])
                last = turn(ps[0:STACK + R, 3, (H + hh) * P:(H + hh + 1) * P], dtw_pad[:, hh])
            last.then_inc(prep_pe, 1)
            for hh in range(H):
                turn(ps[:, 4, hh * (R + BC):(hh + 1) * (R + BC)], xpw[:, hh * P:(hh + 1) * P])
            turn(ps[:, 4, P:P + E], selw[:]).then_inc(prep_pe, 1)
            pe.wait_ge(split_lo, 1)
            pe.wait_ge(small_ready, 1)

            def take(stage, now, job):
                k, n = ring(stage, now, job)
                if stage != "pro" or n > 1:
                    pe.wait_ge(emptied[k], n - 1)
                return k

            def split_products(out, weights, moving):
                for n, (a, b) in enumerate(((0, 0), (0, 1), (1, 0))):
                    last = nc.tensor.matmul(out, weights(a), moving(b), start=(n == 0), stop=(n == 2))
                return last

            def front_xT(stage, now, s):
                pe.wait_ge(xn_ready, s.b + 1)
                for job, src in (("xnT", xn), ("xn2T", xn2)):
                    k = take(stage, now, job)
                    for j in range(T):
                        last = turn(ps[:, RING + k, j * P:(j + 1) * P], src[:, j])
                    last.then_inc(filled[k], 1)

            def front_logits(stage, now, s):
                wait_emptied(pe, stage, now, "xnT")
                k = take(stage, now, "logits")
                for j in range(T):
                    last = split_products(ps[:, RING + k, j * E:(j + 1) * E],
                                          lambda a: xnT[:, s.par, a, j * P:(j + 1) * P], lambda b: sel_t[:, b])
                last.then_inc(filled[k], 1)

            def front_conv(stage, now, s, hh):
                if hh == 0:
                    pe.wait_ge(xn2T_low, s.b + 1)
                k = take(stage, now, f"conv{hh}")
                for tap in range(TAPS):
                    for a, b in ((0, 0), (0, 1), (1, 0)):
                        last = nc.tensor.matmul(ps[:, RING + k], conv_t[:, a, tap, hh], xn2T[:, b, tap:tap + L],
                                                start=(tap + a + b == 0), stop=(tap + a == TAPS))
                last.then_inc(filled[k], 1)

            def front_z(stage, now, part):
                k = take(stage, now, f"z{part}")
                for j in range(2):
                    at = TAPS - 1 + (2 * part + j) * P
                    last = split_products(ps[:, RING + k, j * H * P:(j + 1) * H * P],
                                          lambda a: xn2T[:, a, at:at + P], lambda b: wz_t[:, b])
                last.then_inc(filled[k], 1)

            def front_xdbl(stage, now, s):
                pe.wait_ge(xc_ready, s.b + 1)
                k = take(stage, now, "xdbl")
                for hh in range(H):
                    last = nc.tensor.matmul(ps[0:STACK + R, RING + k], xp_t[:, hh], xc[:, hh], start=(hh == 0),
                                            stop=(hh == H - 1))
                last.then_inc(filled[k], 1)

            def front_gT(stage, now, s):
                pe.wait_ge(g3_ready, s.b + 1)
                k = take(stage, now, "gT")
                for j in range(T):
                    last = nc.tensor.matmul(ps[0:STACK, RING + k, j * P // 2:(j + 1) * P // 2].bitcast(bf16), g3[:, j],
                                            ident16[:], is_transpose=True, start=True, stop=True)
                last.then_inc(filled[k], 1)

            def front_dt(stage, now, s):
                pe.wait_ge(dtr_ready, s.b + 1)
                for hh in range(H):
                    k = take(stage, now, f"dt{hh}")
                    nc.tensor.matmul(ps[:, RING + k], dtw_t[STACK:STACK + R, hh], dtr[STACK:STACK + R],
                                     start=True, stop=True).then_inc(filled[k], 1)

            def back_yT(stage, now, s):
                pe.wait_ge(yz_ready, s.b + 1)
                for hh in range(H):
                    k = take(stage, now, f"yT{hh}")
                    for j in range(T):
                        last = turn(ps[:, RING + k, j * P:(j + 1) * P], yz[:, j, hh * P:(hh + 1) * P])
                    last.then_inc(filled[k], 1)

            def back_m(stage, now):
                wait_emptied(pe, stage, now, "yT0")
                wait_emptied(pe, stage, now, "yT1")
                k = take(stage, now, "m")
                for hh in range(H):
                    last = nc.tensor.matmul(ps[:, RING + k], ow_t[:, hh], yT[:, hh], start=(hh == 0), stop=(hh == H - 1))
                last.then_inc(filled[k], 1)

            def back_glu(stage, now):
                wait_emptied(pe, stage, now, "m")
                for r in (1, 0):
                    k = take(stage, now, f"g{r}")
                    nc.tensor.matmul(ps[:, RING + k], gw_t[:, r], mg[:], start=True, stop=True).then_inc(filled[k], 1)

            def back_fin(stage, now, s):
                wait_emptied(pe, stage, now, "g0")
                pe.wait_ge(moe_s_ready, s.b + 1)
                for part in range(2):
                    k = take(stage, now, f"fin{part}")
                    for j in range(2):
                        at = slice((2 * part + j) * P, (2 * part + j + 1) * P)
                        turn(ps[:, RING + k, j * P:(j + 1) * P], moe_s[:, at])
                        last = turn(ps[:, RING + k, j * P:(j + 1) * P], m2[:, at], start=False,
                                    skip_group_check=True)
                    last.then_inc(filled[k], 1)

            def sum_y(stage, s, i):
                if i == 0:
                    if stage != "first":
                        pe.wait_ge(yz_ready, s.b)
                    for j in range(T):
                        for hh in range(H):
                            nc.tensor.matmul(ps[:, YACC + j // 2, (j % 2 * H + hh) * P:(j % 2 * H + hh + 1) * P],
                                             xc[:, hh, j * P:(j + 1) * P], diag_d[:, hh], start=(j % 2 + hh == 0),
                                             stop=False, skip_group_check=True)
                pe.wait_ge(hc_ready, s.b * N + i + 1)
                for j in range(T):
                    for hh in range(H):
                        last = turn(ps[:, YACC + j // 2, (j % 2 * H + hh) * P:(j % 2 * H + hh + 1) * P],
                                    hC[:, i % 4, hh, j * P:(j + 1) * P], start=False, skip_group_check=True)
                last.then_inc(y_done, 1)

            def sum_moe(stage, s, i):
                if i == 0 and stage != "first":
                    pe.wait_ge(moe_s_ready, s.b)
                pe.wait_ge(hg_ready, s.b * N + i + 1)
                nc.tensor.matmul(ps[:, MOE], val_sb[:, i], hg[:, i % 2], start=(i == 0),
                                 stop=(i == N - 1)).then_inc(moe_done, 1)

            front_xT("pro", None, first_seq)
            front_logits("pro", None, first_seq)
            front_conv("pro", None, first_seq, 0)
            front_conv("pro", None, first_seq, 1)
            front_xdbl("pro", None, first_seq)
            front_dt("pro", None, first_seq)
            front_z("pro", None, 0)
            front_z("pro", None, 1)
            front_gT("pro", None, first_seq)

            def spread_b(s, i, n, reused=True):
                if i == 0:
                    pe.wait_ge(bc_ready, s.b + 1)
                if reused:
                    pe.wait_ge(scan_done, n - 2)
                nc.tensor.matmul(ps[:, 2 - i % 2 * 2], pick_bc[:, i], bc3[:, s.par], start=True,
                                 stop=True).then_inc(b_ready, 1)

            spread_b(first_seq, 0, 1, reused=False)

            def body(stage, s):
                for i in range(N):
                    n = s.b * N + i + 1
                    if i < N - 1:
                        spread_b(s, i + 1, n + 1, reused=stage != "first" or i >= 1)
                    elif stage != "last":
                        spread_b(after(s), 0, n + 1)
                    k = take(stage, s, f"C{i}")
                    nc.tensor.matmul(ps[:, RING + k], pick_bc[:, N + i], bc3[:, s.par], start=True,
                                     stop=True).then_inc(filled[k], 1)
                    if i >= Y_LAG:
                        sum_y(stage, s, i - Y_LAG)
                    elif stage != "first":
                        sum_y(stage, before(s), N + i - Y_LAG)
                    k = take(stage, s, f"S{i}")
                    split_products(ps[:, RING + k],
                                   lambda a: key_t[:, a, 2 * i:2 * i + 2].rearrange("p e f -> p (e f)"),
                                   lambda b: xnT[:, s.par, b]).then_inc(filled[k], 1)
                    if i >= MOE_LAG:
                        sum_moe(stage, s, i - MOE_LAG)
                    elif stage != "first":
                        sum_moe(stage, before(s), N + i - MOE_LAG)
                    k = take(stage, s, f"G{i}")
                    if i == 0:
                        if stage == "first":
                            wait_emptied(pe, "pro", None, "gT")
                        else:
                            wait_emptied(pe, stage, s, "gT", ago=1)
                    nc.tensor.matmul(ps[:, RING + k], pick_g[:, 2 * i:2 * i + 2].rearrange("p e f -> p (e f)"),
                                     gT[:, s.par], start=True, stop=True).then_inc(filled[k], 1)
                    if stage != "first":
                        if i == AT["yT"]:
                            back_yT(stage, s, before(s))
                        if i == AT["m"]:
                            back_m(stage, s)
                        if i == AT["glu"]:
                            back_glu(stage, s)
                        if i == AT["fin"]:
                            back_fin(stage, s, before(s))
                    if stage != "last":
                        if i == AT["xT"]:
                            front_xT(stage, s, after(s))
                        if i == AT["logits"]:
                            front_logits(stage, s, after(s))
                        for hh in range(H):
                            if i == AT[f"conv{hh}"]:
                                front_conv(stage, s, after(s), hh)
                        if i == AT["xdbl"]:
                            front_xdbl(stage, s, after(s))
                        if i == AT["dt"]:
                            front_dt(stage, s, after(s))
                        for part in range(2):
                            if i == AT[f"z{part}"]:
                                front_z(stage, s, part)
                        if i == AT["gT"]:
                            front_gT(stage, s, after(s))

            walk(pe, body)
            for i in range(N - Y_LAG, N):
                sum_y("last", last_seq, i)
            for i in range(N - MOE_LAG, N):
                sum_moe("last", last_seq, i)
            back_yT("epi", None, last_seq)
            back_m("epi", None)
            back_glu("epi", None)
            back_fin("epi", None, last_seq)


_INS = ["L0_attn_x", "L0_attn_ln_g", "L0_attn_ln_b", "L0_attn_in_proj_w", "L0_attn_conv_w", "L0_attn_conv_b",
        "L0_attn_x_proj_w", "L0_attn_dt_proj_w", "L0_attn_dt_proj_b", "L0_attn_A_log", "L0_attn_D",
        "L0_attn_out_proj_w", "L0_attn_glu_w", "L0_attn_glu_b", "L0_ffn_expert_sel", "L0_ffn_keys", "L0_ffn_values"]


def kernel(**inputs):
    import numpy as _np
    import concourse.bacc as _bacc
    from concourse import mybir as _mybir
    from concourse.bass_utils import run_bass_kernel_spmd as _run

    nc = _bacc.Bacc("TRN2", target_bir_lowering=False, num_devices=1)
    arrays, args = {}, []
    for name in _INS:
        a = _np.ascontiguousarray(inputs[name])
        arrays[f"in_{name}_dram"] = a
        args.append(nc.dram_tensor(f"in_{name}_dram", a.shape, _mybir.dt.from_np(a.dtype), kind="ExternalInput").ap())
    shape = inputs["L0_attn_x"].shape
    args.append(nc.dram_tensor("out_dram", shape, _mybir.dt.float32, kind="ExternalOutput").ap())
    mamba_moe(nc, *args)
    r = _run(nc, [arrays], core_ids=[0])
    return r.results[0]["out_dram"]
```

```python
import concourse.bass as bass
from concourse import mybir
from contextlib import ExitStack
from collections import namedtuple

P = 128
Seq = namedtuple("Seq", "b par half")


def after(s):
    return Seq(s.b + 1, 1 - s.par, s.half + s.par)


def before(s):
    return Seq(s.b - 1, 1 - s.par, s.half - (1 - s.par))


def mamba_moe(nc, x, ln_g, ln_b, in_w, conv_w, conv_b, xp_w, dtp_w, dtp_b, a_log, d_skip, out_w,
              glu_w, glu_b, sel_w, keys, values, out):
    fp32, f32r, bf16 = mybir.dt.float32, mybir.dt.float32r, mybir.dt.bfloat16
    ALU, ACT = mybir.AluOpType, mybir.ActivationFunctionType
    B, L, D = x.shape
    H = in_w.shape[0] // 2 // P
    TAPS = conv_w.shape[2]
    N = a_log.shape[1]
    R = dtp_w.shape[1]
    E, _, F = keys.shape
    T = L // P
    TOP = 4
    CONVS = 2 * H
    GATE_LAG, Y_LAG, MOE_LAG = 1, 2, 2
    C_STORE = 4
    LOADS = 10
    EPS = 1e-5
    BC = 2 * N
    STACK = 3 * BC
    PAIRS = E * F // P
    assert PAIRS == N and STACK == 3 * E and T * P == L and L == 512

    AT = {"yT": 5, "m": 22, "glu": 33, "fin": 34, "xT": 7, "logits": 36, "conv0": 11, "conv1": 11, "conv2": 12,
          "conv3": 12, "xdbl": 25, "dt": 29, "z0": 41, "z1": 43, "gT": 41}
    AT_ACT = {"moe": 5, "exp": 32, "ln": 34}
    AT_DVE = {"yz": 4, "glu": 35, "fin": 37, "stats": 1, "xn": 7, "xT": 9, "gates": 40, "xc": 16, "bc": 28,
              "bc_low": 30, "round": 35, "z0": 42, "z1": 44, "dt": 41}
    AT_POOL = {"norm": 1, "rest": 35, "sum": 36, "residual": 36}
    JOBS = {"yT": ["yT0", "yT1"], "m": ["m"], "glu": ["g1", "g0"], "fin": ["fin0", "fin1"], "xT": ["xnT", "xn2T"],
            "dt": ["dt0", "dt1"]}
    MISC = {i: [job for piece in AT if AT[piece] == i for job in JOBS.get(piece, [piece])] for i in range(3 * N)}
    BACK = {"yT0", "yT1", "m", "g1", "g0", "fin0", "fin1"}
    FRONT = ["xnT", "xn2T", "conv0", "conv1", "conv2", "conv3", "xdbl", "logits", "dt0", "dt1", "z0", "z1", "gT"]
    ORDER = [j for i in range(N) for j in MISC[3 * i] + [f"S{i}"] + MISC[3 * i + 1] + [f"G{i}"] + MISC[3 * i + 2]]
    FIRST = [j for j in ORDER if j not in BACK]
    LAST = [j for j in ORDER if j not in FRONT]
    TAIL = [j for j in ORDER if j in BACK]
    LOOPED = len(FRONT) + len(FIRST)
    assert len(ORDER) % 2 == LOOPED % 2 == 0

    def ring(stage, now, job, ago=0):
        table = {"pro": FRONT, "first": FIRST, "body": ORDER, "last": LAST, "epi": TAIL}[stage]
        at = ORDER.index(job) - len(ORDER) if ago else table.index(job)
        if stage == "body" or stage == "last":
            return at % 2, (now.b - 1) * (len(ORDER) // 2) + LOOPED // 2 + at // 2 + 1
        at += {"pro": 0, "first": len(FRONT), "epi": LOOPED + len(ORDER) * (B - 2) + len(LAST)}[stage]
        return at % 2, at // 2 + 1

    ctx = ExitStack()
    with ctx:
        def sb(name, shape, dt=fp32):
            return ctx.enter_context(nc.sbuf_tensor(name, shape, dt))

        def sem(name):
            return ctx.enter_context(nc.semaphore(name))

        hC = sb("hC", [P, 4, H, L])
        win = hC[:, 2, 0].rearrange("p (r d) -> p r d", d=D)
        key_sb = hC[:, 0:2].rearrange("p a h (e f) -> p (a h e) f", f=F)
        xpw = sb("xpw", [R + BC, H * P])
        dtw = sb("dtw", [P, H, R])
        ow = hC[:, 2, 1, 0:H * P]
        gw = hC[:, 2, 1, H * P:].rearrange("p (r d) -> p r d", d=D)
        selw = sb("selw", [E, D])
        val_sb = sb("val_sb", [P, PAIRS, D])
        alog = sb("alog", [P, H, N])
        lng = sb("lng", [P, 1])
        lnb = sb("lnb", [P, 1])
        cw = sb("cw", [P, H, TAPS])
        cb = sb("cb", [P, H])
        dtb = sb("dtb", [P, H])
        dsk = sb("dsk", [P, H])
        glb = sb("glb", [P, 2])
        ones = sb("ones", [P, P])
        ident = sb("ident", [P, P])
        ident16 = sb("ident16", [P, P], bf16)
        win_tap = hC[:, 3].rearrange("p h (k d) -> p (h k) d", d=D)
        dtw_pad = sb("dtw_pad", [P, H, STACK + R])
        conv_t = sb("conv_t", [P, 2, TAPS, H, P], f32r)
        wz_t = sb("wz_t", [P, 2, H * P], f32r)
        key_t = sb("key_t", [P, 2, E, F], f32r)
        sel_t = sb("sel_t", [P, 2, E], f32r)
        ow_t = sb("ow_t", [P, H, D])
        gw_t = sb("gw_t", [P, 2, D])
        dtw_t = sb("dtw_t", [P, H, P])
        xp_t = sb("xp_t", [P, H, STACK + R])
        diag_d = sb("diag_d", [P, H, P])
        a_neg = sb("a_neg", [P, H, N])
        cb_half = sb("cb_half", [P, H])
        glb_half = sb("glb_half", [P, 1])
        pick = sb("pick", [P, BC])
        pick_b = sb("pick_b", [STACK, N, P], bf16)
        pick_g = sb("pick_g", [STACK, E, F], bf16)
        xt = sb("xt", [P, 2, T, D])
        stats = sb("stats", [P, T, 6])
        mv = sb("mv", [P, T, 2])
        rstd = sb("rstd", [P, 2, T])
        vtmp = sb("vtmp", [P, T])
        minus_half = sb("minus_half", [P, T])
        eps = sb("eps", [P, T])
        xn = sb("xn", [P, T, D])
        xn2 = sb("xn2", [P, T, D])
        xres = sb("xres", [P, 2, T, D])
        xnT = sb("xnT", [P, 2, 2, L], f32r)
        xn2T = sb("xn2T", [P, 2, TAPS - 1 + L], f32r)
        cpre = drelu = sb("conv_then_relu", [P, H, L])
        cth = dln = sb("tanh_then_log", [P, H, L])
        xc = sb("xc", [P, H, L])
        zth = sb("tanh_z_then_yT", [P, T, H * P])
        sz = sb("sz", [P, 2, T, H * P])
        lth = sb("lth", [P, T, E])
        gates = sb("gates", [P, T, E + TOP])
        gates_left = sb("gates_left", [P, T, E + TOP])
        top8 = sb("top8", [P, T, 8])
        gtop = sb("gtop", [P, T, E])
        grest = sb("grest", [P, T, E])
        g3 = sb("g3", [P, T, STACK], bf16)
        gT = sb("gT", [STACK, 2, L], bf16)
        bc3 = sb("bc3", [STACK, 2, L], bf16)
        rows = sb("rows", [P, L])
        bcrest, crow, dtr = rows[0:2 * BC], rows[STACK - N:STACK], rows[STACK:STACK + R]
        dexp = sb("dexp", [P, H, L])
        drest = sb("rest_then_yz", [P, H, L])
        dt = sb("dt", [P, 2, H, L])
        dtu = sb("dtu", [P, 2, H, L])
        dA = sb("dA", [P, 2, H, L])
        h = sb("h", [P, 2, H, L])
        relu_s = sb("relu_s", [P, 4, L])
        Cs = sb("Cs", [P, 2, 2, L])
        Gs = sb("Gs", [P, 4, L])
        hg = sb("hg", [P, 2, L])
        moe_s = sb("moe_s", [P, L])
        yz = drest[:].rearrange("p h l -> p (h l)").rearrange("p (t c) -> p t c", t=T)
        yT = zth[:].rearrange("p t (h c) -> p (t h c)", h=H).rearrange("p (h l) -> p h l", h=H)
        mg = sb("mg", [P, L])
        th2 = xn2T_full = sb("th2", [P, L])
        m2 = xn2[:].rearrange("p t d -> p (t d)")
        outb = sb("outb", [P, 2, T, D])

        ps = ctx.enter_context(nc.psum_tensor("ps", [P, 8, 512], fp32))
        RING, MOE, YACC = 3, 5, 6

        split_hi, split_lo = sem("split_hi"), sem("split_lo")
        conv_in, experts_in, tables_ready = sem("conv_in"), sem("experts_in"), sem("tables_ready")
        w_in, ident_ready, halves_ready = sem("w_in"), sem("ident_ready"), sem("halves_ready")
        pads_ready, prep_pe = sem("pads_ready"), sem("prep_pe")
        a_exp_ready, small_ready = sem("a_exp_ready"), sem("small_ready")
        x_in = [sem("x_in0"), sem("x_in1")]
        stored = [sem("stored0"), sem("stored1")]
        c_stored, c_in = sem("c_stored"), [sem("c_in0"), sem("c_in1")]
        filled = [sem("filled0"), sem("filled1")]
        emptied = [sem("emptied0"), sem("emptied1")]
        b_ready, dbu_ready, da_ready = sem("b_ready"), sem("dbu_ready"), sem("da_ready")
        hg_ready = sem("hg_ready")
        scan_done, hc_ready, y_done, moe_done = sem("scan_done"), sem("hc_ready"), sem("y_done"), sem("moe_done")
        exp_ready = sem("exp_ready")
        rounded_ready, rest_ready, sum_ready = sem("rounded_ready"), sem("rest_ready"), sem("sum_ready")
        mv_ready, rstd_ready, xn_ready, xres_ready = sem("mv_ready"), sem("rstd_ready"), sem("xn_ready"), sem("xres_ready")
        g3_ready, xc_ready, hi_ready, dtr_ready = sem("g3_ready"), sem("xc_ready"), sem("hi_ready"), sem("dtr_ready")
        xnT_hi, xn2T_low = sem("xnT_hi"), sem("xn2T_low")
        zth_ready, bc_ready, ln_ready = sem("zth_ready"), sem("bc_ready"), sem("ln_ready")
        dt_ready, dtu_ready = sem("dt_ready"), sem("dtu_ready")
        moe_s_ready, yz_ready, m2_ready = sem("moe_s_ready"), sem("yz_ready"), sem("m2_ready")

        c_dram = nc.dram_tensor("c_rows", (2, N, L), fp32, kind="Internal").ap()
        x_v = x.rearrange("b (j p) d -> b p j d", p=P)
        out_v = out.rearrange("b (j p) d -> b p j d", p=P)
        first_seq, last_seq = Seq(0, 0, 0), Seq(B - 1, (B - 1) % 2, (B - 1) // 2)

        def walk(eng, body):
            body("first", first_seq)
            with eng.Fori(0, (B - 2) // 2) as pair:
                body("body", Seq(2 * pair + 1, 1, pair))
                body("body", Seq(2 * pair + 2, 0, pair + 1))
            body("last", last_seq)

        def wait_filled(eng, stage, now, job):
            k, n = ring(stage, now, job)
            eng.wait_ge(filled[k], n)
            return k

        def wait_emptied(eng, stage, now, job, ago=0):
            k, n = ring(stage, now, job, ago)
            eng.wait_ge(emptied[k], n)

        block = ctx.enter_context(nc.Block())

        @block.sync
        def _(sp):
            def load_x(s):
                sp.dma_start(xt[:, s.par], x_v[s.b]).then_inc(x_in[s.par], 16)

            def store_out(stage, now, s):
                wait_emptied(sp, stage, now, "fin1")
                sp.dma_start(out_v[s.b], outb[:, s.par]).then_inc(stored[s.par], 16)

            load_x(first_seq)
            sp.dma_start(win[:], in_w.rearrange("(r p) d -> p r d", p=P)).then_inc(conv_in, 16)
            with nc.allow_non_contiguous_dma(reason="vectors of 128 and 256 elements, loaded once"):
                sp.dma_start(cw[:], conv_w.rearrange("(h p) o k -> p h (o k)", p=P)).then_inc(conv_in, 16)
                sp.dma_start(lng[:], ln_g.unsqueeze(1)).then_inc(conv_in, 16)
                sp.dma_start(lnb[:], ln_b.unsqueeze(1)).then_inc(conv_in, 16)
            loads = [
                (xpw, xp_w), (dtw, dtp_w.rearrange("(h p) r -> p h r", p=P)),
                (ow, out_w), (gw, glu_w.rearrange("(r p) d -> p r d", p=P)), (selw, sel_w),
                (alog, a_log.rearrange("(h p) n -> p h n", p=P)),
                (cb, conv_b.rearrange("(h p) -> p h", p=P)), (dtb, dtp_b.rearrange("(h p) -> p h", p=P)),
                (dsk, d_skip.rearrange("(h p) -> p h", p=P)), (glb, glu_b.rearrange("(h p) -> p h", p=P)),
            ]
            assert len(loads) == LOADS
            with nc.allow_non_contiguous_dma(reason="vectors of 256 elements, loaded once"):
                for to, what in loads:
                    sp.dma_start(to[:], what).then_inc(w_in, 16)
            sp.dma_start(key_sb[:], keys.rearrange("e d f -> d e f")).then_inc(experts_in, 16)
            sp.dma_start(val_sb[:], values.rearrange("(i a) f v -> (a f) i v", a=P // F)).then_inc(experts_in, 16)

            def store_c(s):
                sp.wait_ge(dtr_ready, s.b + 1)
                sp.dma_start(c_dram[s.par], crow).then_inc(c_stored, 16)

            def load_c(s, k):
                rows_2 = c_dram[s.par, 2 * k:2 * k + 2].rearrange("n l -> (n l)").unsqueeze(0).broadcast_to([P, 2 * L])
                sp.dma_start(Cs[:, k % 2].rearrange("p n l -> p (n l)"), rows_2).then_inc(c_in[k % 2], 16)

            store_c(first_seq)
            sp.wait_ge(c_stored, 32)
            load_c(first_seq, 0)

            def body(stage, s):
                if stage == "first":
                    load_x(after(s))
                elif stage == "body":
                    sp.wait_ge(xres_ready, s.b)
                    load_x(after(s))
                for k in range(N // 2):
                    if k == C_STORE and stage != "last":
                        store_c(after(s))
                    if k == N // 2 - 1:
                        if stage != "first":
                            store_out(stage, s, before(s))
                        if stage == "last":
                            break
                    if stage != "first" or k >= 1:
                        sp.wait_ge(hc_ready, s.b * N + 2 * k)
                    if k < N // 2 - 1:
                        load_c(s, k + 1)
                    else:
                        load_c(after(s), 0)

            walk(sp, body)
            store_out("epi", None, last_seq)
            sp.wait_ge(stored[0], 16 * (B // 2 + 1))
            sp.wait_ge(stored[1], 16 * (B // 2 + 1))

        @block.gpsimd
        def _(pool):
            nc.gpsimd.memset(ones[:], 1.0)
            nc.gpsimd.memset(minus_half[:], -0.5)
            nc.gpsimd.memset(eps[:], EPS)
            nc.gpsimd.drain()
            nc.gpsimd.affine_select(out=ident[:], in_=ones[:], compare_op=ALU.is_equal, fill=0.0, base=0,
                                    pattern=[[-1, P]], channel_multiplier=1).then_inc(ident_ready, 1)

            def norm_scales(s):
                pool.wait_ge(mv_ready, s.b + 1)
                nc.gpsimd.tensor_tensor(vtmp[:], mv[:, :, 1], eps[:], ALU.add)
                nc.gpsimd.drain()
                nc.gpsimd.tensor_tensor(rstd[:, 0], vtmp[:], minus_half[:], ALU.pow)
                nc.gpsimd.drain()
                nc.gpsimd.tensor_tensor(vtmp[:], mv[:, :, 1], rstd[:, 0], ALU.mult)
                nc.gpsimd.drain()
                nc.gpsimd.tensor_tensor(vtmp[:], vtmp[:], rstd[:, 0], ALU.mult)
                nc.gpsimd.drain()
                nc.gpsimd.tensor_scalar(vtmp[:], vtmp[:], EPS, None, ALU.add)
                nc.gpsimd.drain()
                nc.gpsimd.tensor_tensor(rstd[:, 1], vtmp[:], minus_half[:], ALU.pow).then_inc(rstd_ready, 1)

            def residual(s):
                pool.wait_ge(xn_ready, s.b + 1)
                nc.gpsimd.tensor_tensor(xres[:, s.par], xt[:, s.par], xn[:], ALU.add).then_inc(xres_ready, 1)

            def softplus_rest(s):
                pool.wait_ge(rounded_ready, s.b + 1)
                nc.gpsimd.tensor_tensor(drest[:], dexp[:], drest[:], ALU.subtract).then_inc(rest_ready, 1)

            def softplus_sum(s):
                pool.wait_ge(ln_ready, s.b + 1)
                nc.gpsimd.tensor_tensor(dln[:], dln[:], drelu[:], ALU.add).then_inc(sum_ready, 1)

            def gate(stage, now, i, n, ago=0, reused=True):
                wait_emptied(pool, stage, now, f"G{i}", ago)
                if reused:
                    pool.wait_ge(moe_done, n - 2)
                nc.gpsimd.tensor_tensor(hg[:, i % 2], relu_s[:, i % 4], Gs[:, i % 4], ALU.mult).then_inc(hg_ready, 1)

            norm_scales(first_seq)
            residual(first_seq)
            softplus_rest(first_seq)
            softplus_sum(first_seq)

            def pieces(stage, s, at):
                if stage != "last":
                    if at == AT_POOL["norm"]:
                        norm_scales(after(s))
                    if at == AT_POOL["rest"]:
                        softplus_rest(after(s))
                    if at == AT_POOL["sum"]:
                        softplus_sum(after(s))
                    if at == AT_POOL["residual"]:
                        if stage != "first":
                            wait_emptied(pool, stage, s, "fin1")
                        residual(after(s))

            def body(stage, s):
                for i in range(N):
                    n = s.b * N + i + 1
                    pieces(stage, s, 3 * i)
                    if i >= GATE_LAG:
                        gate(stage, s, i - GATE_LAG, n - GATE_LAG, reused=stage != "first" or i >= GATE_LAG + 2)
                    elif stage != "first":
                        gate(stage, s, N + i - GATE_LAG, n - GATE_LAG, ago=1)
                    pieces(stage, s, 3 * i + 1)
                    if i == N - 4 and stage != "last":
                        pool.wait_ge(c_stored, 16 * s.b + 48)
                    pool.wait_ge(scan_done, n)
                    if i % 2 == 0:
                        pool.wait_ge(c_in[i // 2 % 2], 16 * (s.b * (N // 4) + i // 4 + 1))
                    if stage != "first" or i >= 4:
                        pool.wait_ge(y_done, n - 4)
                    c_row = Cs[:, i // 2 % 2, i % 2].unsqueeze(1).broadcast_to([P, H, L])
                    nc.gpsimd.tensor_tensor(hC[:, i % 4], h[:, i % 2], c_row, ALU.mult).then_inc(hc_ready, 1)
                    pieces(stage, s, 3 * i + 2)

            walk(pool, body)
            for i in range(N - GATE_LAG, N):
                gate("last", last_seq, i, (B - 1) * N + i + 1)

        @block.scalar
        def _(act):
            def to_sbuf(dst, src, scale=1.0):
                return nc.scalar.activation(dst, src, ACT.Copy, scale=scale)

            def front_xT(stage, now, s):
                k = wait_filled(act, stage, now, "xnT")
                to_sbuf(xnT[:, s.par, 0], ps[:, RING + k]).then_inc(xnT_hi, 1)
                k = wait_filled(act, stage, now, "xn2T")
                nc.scalar.activation(xn2T_full[:], ps[:, RING + k], ACT.Identity, bias=lnb[:, 0:1],
                                     scale=lng[:, 0:1])
                nc.scalar.activation(xn2T[:, 0, TAPS - 1:], ps[:, RING + k], ACT.Identity, bias=lnb[:, 0:1],
                                     scale=lng[:, 0:1]).then_inc(emptied[k], 1)

            def front_logits(stage, now):
                k = wait_filled(act, stage, now, "logits")
                nc.scalar.activation(lth[:], ps[:, RING + k, 0:T * E].rearrange("p (j e) -> p j e", j=T), ACT.Tanh,
                                     scale=0.5).then_inc(emptied[k], 1)

            def front_conv(stage, now, part):
                hh, half = part // 2, slice(part % 2 * L // 2, (part % 2 + 1) * L // 2)
                k = wait_filled(act, stage, now, f"conv{part}")
                nc.scalar.activation(cpre[:, hh, half], ps[:, RING + k, 0:L // 2], ACT.Identity,
                                     bias=cb_half[:, hh:hh + 1])
                nc.scalar.activation(cth[:, hh, half], ps[:, RING + k, 0:L // 2], ACT.Tanh,
                                     bias=cb_half[:, hh:hh + 1]).then_inc(emptied[k], 1)

            def front_z(stage, now, part):
                k = wait_filled(act, stage, now, f"z{part}")
                nc.scalar.activation(zth[:, 2 * part:2 * part + 2], ps[:, RING + k].rearrange("p (j c) -> p j c", j=2),
                                     ACT.Tanh).then_inc(zth_ready, 1)

            def front_xdbl(stage, now, s):
                k = wait_filled(act, stage, now, "xdbl")
                to_sbuf(bc3[:, s.par], ps[0:STACK, RING + k]).then_inc(hi_ready, 1)
                act.wait_ge(c_stored, 16 * s.b + 16)
                to_sbuf(rows[2 * BC:STACK + R], ps[2 * BC:STACK + R, RING + k]).then_inc(dtr_ready, 1)

            def front_gT(stage, now, s):
                k = wait_filled(act, stage, now, "gT")
                to_sbuf(gT[:, s.par], ps[0:STACK, RING + k, 0:L // 2].bitcast(bf16)).then_inc(emptied[k], 1)

            def front_dt(stage, now):
                for hh in range(H):
                    k = wait_filled(act, stage, now, f"dt{hh}")
                    nc.scalar.activation(dexp[:, hh], ps[:, RING + k], ACT.Abs, bias=dtb[:, hh:hh + 1])
                    nc.scalar.activation(drelu[:, hh], ps[:, RING + k], ACT.Relu,
                                         bias=dtb[:, hh:hh + 1]).then_inc(emptied[k], 1)

            def front_exp(s):
                nc.scalar.drain()
                nc.scalar.activation(dexp[:], dexp[:], ACT.Exp, scale=-1.0).then_inc(exp_ready, 1)

            def front_ln(s):
                act.wait_ge(exp_ready, s.b + 1)
                nc.scalar.activation(dln[:], dexp[:], ACT.Ln, bias=1.0).then_inc(ln_ready, 1)

            def back_moe(s):
                act.wait_ge(moe_done, (s.b + 1) * N)
                to_sbuf(moe_s[:], ps[:, MOE]).then_inc(moe_s_ready, 1)

            def back_yT(stage, now):
                for hh in range(H):
                    k = wait_filled(act, stage, now, f"yT{hh}")
                    to_sbuf(yT[:, hh], ps[:, RING + k]).then_inc(emptied[k], 1)

            def back_gelu(stage, now):
                k = wait_filled(act, stage, now, "m")
                nc.scalar.activation(mg[:], ps[:, RING + k], ACT.Gelu).then_inc(emptied[k], 1)

            def back_glu(stage, now):
                k = wait_filled(act, stage, now, "g1")
                nc.scalar.activation(th2[:], ps[:, RING + k], ACT.Tanh, bias=glb_half[:, 0:1],
                                     scale=0.5).then_inc(emptied[k], 1)

            act.wait_ge(prep_pe, 1)
            to_sbuf(conv_t[:, 0, 0:2], ps[:, 0].rearrange("p (k h c) -> p k h c", k=2, h=H))
            act.wait_ge(prep_pe, 2)
            to_sbuf(conv_t[:, 0, 2:4], ps[:, 1].rearrange("p (k h c) -> p k h c", k=2, h=H)).then_inc(split_hi, 1)
            act.wait_ge(conv_in, 64)
            front_xT("pro", None, first_seq)
            act.wait_ge(w_in, 16 * LOADS)
            nc.scalar.activation(a_neg[:], alog[:], ACT.Exp).then_inc(a_exp_ready, 1)
            act.wait_ge(small_ready, 1)
            for part in range(CONVS):
                front_conv("pro", None, part)
            act.wait_ge(prep_pe, 3)
            to_sbuf(wz_t[:, 0], ps[:, 2, 0:2 * P], scale=0.5)
            to_sbuf(ow_t[:], ps[:, 2, 2 * P:4 * P].rearrange("p (h m) -> p h m", h=H))
            act.wait_ge(prep_pe, 4)
            to_sbuf(gw_t[:], ps[:, 5, 0:2 * P].rearrange("p (h m) -> p h m", h=2))
            to_sbuf(dtw_t[STACK:STACK + R], ps[STACK:STACK + R, 5, 2 * P:4 * P].rearrange("p (h m) -> p h m", h=H))
            act.wait_ge(prep_pe, 5)
            xp_ps = ps[:, 6, 0:H * (R + BC)].rearrange("p (h c) -> p h c", h=H)
            for k in range(3):
                to_sbuf(xp_t[:, :, k * BC:(k + 1) * BC], xp_ps[:, :, R:R + BC])
            to_sbuf(xp_t[:, :, STACK:STACK + R], xp_ps[:, :, 0:R])
            to_sbuf(sel_t[:, 0], ps[:, 6, P:P + E]).then_inc(split_hi, 1)
            front_xdbl("pro", None, first_seq)
            front_logits("pro", None)
            front_dt("pro", None)
            front_exp(first_seq)
            front_ln(first_seq)
            front_z("pro", None, 0)
            front_z("pro", None, 1)
            front_gT("pro", None, first_seq)

            def decay(s, i, n, reused=True):
                if i == 0:
                    act.wait_ge(dt_ready, s.b + 1)
                if reused:
                    act.wait_ge(scan_done, n - 2)
                for hh in range(H):
                    last = nc.scalar.activation(dA[:, i % 2, hh, 1:L], dt[:, s.par, hh, 1:L], ACT.Exp,
                                                scale=a_neg[:, hh, i:i + 1])
                last.then_inc(da_ready, 1)

            decay(first_seq, 0, 1, reused=False)

            def pieces(stage, s, at):
                if stage != "first":
                    if at == AT_ACT["moe"]:
                        back_moe(before(s))
                    if at == AT["yT"]:
                        back_yT(stage, s)
                    if at == AT["m"]:
                        back_gelu(stage, s)
                    if at == AT["glu"]:
                        back_glu(stage, s)
                if stage != "last":
                    if at == AT["xT"]:
                        front_xT(stage, s, after(s))
                    if at == AT["logits"]:
                        front_logits(stage, s)
                    for part in range(CONVS):
                        if at == AT[f"conv{part}"]:
                            front_conv(stage, s, part)
                    if at == AT["xdbl"]:
                        front_xdbl(stage, s, after(s))
                    if at == AT["dt"]:
                        front_dt(stage, s)
                    if at == AT_ACT["exp"]:
                        front_exp(after(s))
                    if at == AT_ACT["ln"]:
                        front_ln(after(s))
                    for part in range(2):
                        if at == AT[f"z{part}"]:
                            front_z(stage, s, part)
                    if at == AT["gT"]:
                        front_gT(stage, s, after(s))

            def body(stage, s):
                for i in range(N):
                    n = s.b * N + i + 1
                    pieces(stage, s, 3 * i)
                    if i < N - 1:
                        decay(s, i + 1, n + 1, reused=stage != "first" or i >= 1)
                    elif stage != "last":
                        decay(after(s), 0, n + 1)
                    k = wait_filled(act, stage, s, f"S{i}")
                    if stage != "first" or i >= 4:
                        act.wait_ge(hg_ready, n - 4)
                    nc.scalar.activation(relu_s[:, i % 4], ps[:, RING + k], ACT.Relu).then_inc(emptied[k], 1)
                    pieces(stage, s, 3 * i + 1)
                    k = wait_filled(act, stage, s, f"G{i}")
                    to_sbuf(Gs[:, i % 4], ps[:, RING + k]).then_inc(emptied[k], 1)
                    pieces(stage, s, 3 * i + 2)

            walk(act, body)
            back_moe(last_seq)
            back_yT("epi", None)
            back_gelu("epi", None)
            back_glu("epi", None)

        @block.vector
        def _(dve):
            def front_stats(s):
                dve.wait_ge(x_in[s.par], 16 * (s.half + 1))
                for j in range(T):
                    nc.vector.bn_stats(stats[:, j], xt[:, s.par, j])
                nc.vector.drain()
                for j in range(T):
                    last = nc.vector.bn_aggr(mv[:, j], stats[:, j])
                last.then_inc(mv_ready, 1)

            def front_xn(s):
                dve.wait_ge(rstd_ready, s.b + 1)
                for j in range(T):
                    nc.vector.tensor_scalar(xn[:, j], xt[:, s.par, j], mv[:, j, 0:1], rstd[:, 0, j:j + 1],
                                            ALU.subtract, ALU.mult)
                nc.vector.drain()
                for j in range(T):
                    last = nc.vector.tensor_scalar(xn2[:, j], xn[:, j], rstd[:, 1, j:j + 1], None, ALU.mult)
                last.then_inc(xn_ready, 1)

            def front_xT_low(stage, now, s):
                dve.wait_ge(xnT_hi, s.b + 1)
                k, _ = ring(stage, now, "xnT")
                nc.vector.tensor_tensor(xnT[:, s.par, 1], ps[:, RING + k], xnT[:, s.par, 0],
                                        ALU.subtract).then_inc(emptied[k], 1)
                wait_emptied(dve, stage, now, "xn2T")
                nc.vector.tensor_tensor(xn2T[:, 1, TAPS - 1:], xn2T_full[:], xn2T[:, 0, TAPS - 1:],
                                        ALU.subtract).then_inc(xn2T_low, 1)

            def front_gates(stage, now):
                wait_emptied(dve, stage, now, "logits")
                nc.vector.tensor_scalar(gates[:, :, 0:E], lth[:], 0.5, 0.5, ALU.mult, ALU.add)
                nc.vector.drain()
                for j in range(T):
                    nc.vector.max(top8[:, j], gates[:, j, 0:E])
                nc.vector.drain()
                nc.vector.memset(top8[:, :, TOP:], 2.0)
                nc.vector.drain()
                for j in range(T):
                    nc.vector.match_replace(out=gates_left[:, j], in_to_replace=top8[:, j], in_values=gates[:, j],
                                            imm_value=0.0)
                nc.vector.drain()
                nc.vector.tensor_tensor(gtop[:], gates[:, :, 0:E], gates_left[:, :, 0:E], ALU.subtract)
                nc.vector.drain()
                nc.vector.tensor_copy(g3[:, :, 2 * E:], gtop[:])
                nc.vector.drain()
                nc.vector.tensor_tensor(grest[:], gtop[:], g3[:, :, 2 * E:], ALU.subtract)
                nc.vector.drain()
                nc.vector.tensor_copy(g3[:, :, E:2 * E], grest[:])
                nc.vector.drain()
                nc.vector.tensor_tensor(g3[:, :, 0:E], grest[:], g3[:, :, E:2 * E], ALU.subtract).then_inc(g3_ready, 1)

            def front_xc(stage, now, s):
                wait_emptied(dve, stage, now, "conv3")
                nc.vector.scalar_tensor_tensor(xc[:], cth[:], 1.0, cpre[:], ALU.add, ALU.mult).then_inc(xc_ready, 1)

            def front_sz(stage, now, s, part):
                dve.wait_ge(zth_ready, 2 * s.b + part + 1)
                k, _ = ring(stage, now, f"z{part}")
                nc.vector.scalar_tensor_tensor(sz[:, s.par, 2 * part:2 * part + 2], zth[:, 2 * part:2 * part + 2], 1.0,
                                               ps[:, RING + k].rearrange("p (j c) -> p j c", j=2),
                                               ALU.add, ALU.mult).then_inc(emptied[k], 1)

            def front_bc(stage, now, s):
                dve.wait_ge(hi_ready, s.b + 1)
                dve.wait_ge(dtr_ready, s.b + 1)
                k, _ = ring(stage, now, "xdbl")
                nc.vector.tensor_tensor(bcrest, ps[0:2 * BC, RING + k], bc3[0:2 * BC, s.par],
                                        ALU.subtract).then_inc(emptied[k], 1)

            def front_bc_low(s):
                nc.vector.drain()
                nc.vector.tensor_copy(bc3[0:2 * BC, s.par], bcrest)
                nc.vector.drain()
                nc.vector.tensor_tensor(bc3[0:BC, s.par], bcrest[0:BC], bc3[0:BC, s.par],
                                        ALU.subtract).then_inc(bc_ready, 1)

            def front_round(s):
                dve.wait_ge(exp_ready, s.b + 1)
                nc.vector.tensor_scalar(drest[:], dexp[:], 1.0, 1.0, ALU.add, ALU.subtract).then_inc(rounded_ready, 1)

            def front_dt(s):
                dve.wait_ge(sum_ready, s.b + 1)
                dve.wait_ge(rest_ready, s.b + 1)
                nc.vector.tensor_tensor(dt[:, s.par], dln[:], drest[:], ALU.add).then_inc(dt_ready, 1)
                nc.vector.drain()
                nc.vector.tensor_tensor(dtu[:, s.par], dt[:, s.par], xc[:], ALU.mult).then_inc(dtu_ready, 1)

            def back_yz(s):
                dve.wait_ge(y_done, (s.b + 1) * N)
                nc.vector.tensor_tensor(yz[:], ps[:, YACC:YACC + 2].rearrange("p k (j c) -> p (k j) c", j=2), sz[:, s.par],
                                        ALU.mult).then_inc(yz_ready, 1)

            def back_glu(stage, now):
                wait_emptied(dve, stage, now, "g1")
                nc.vector.tensor_scalar(th2[:], th2[:], 0.5, 0.5, ALU.mult, ALU.add)
                nc.vector.drain()
                k = wait_filled(dve, stage, now, "g0")
                nc.vector.scalar_tensor_tensor(m2, ps[:, RING + k], glb[:, 0:1], th2[:], ALU.add,
                                               ALU.mult).then_inc(emptied[k], 1)

            def back_out(stage, now, s):
                dve.wait_ge(xres_ready, s.b + 1)
                dve.wait_ge(stored[s.par], 16 * (s.half + 1))
                for part in range(2):
                    k = wait_filled(dve, stage, now, f"fin{part}")
                    two = slice(2 * part, 2 * part + 2)
                    nc.vector.tensor_tensor(outb[:, s.par, two],
                                            ps[:, RING + k, 0:2 * P].rearrange("p (j d) -> p j d", j=2),
                                            xres[:, s.par, two], ALU.add).then_inc(emptied[k], 1)

            nc.vector.memset(dA[:, :, :, 0:1], 0.0)
            nc.vector.memset(xn2T[:, :, 0:TAPS - 1].bitcast(fp32), 0.0)
            nc.vector.memset(gates[:, :, E:], 2.0)
            nc.vector.memset(dtw_pad[:], 0.0)
            front_stats(first_seq)
            dve.wait_ge(conv_in, 64)
            for k in range(TAPS):
                for hh in range(H):
                    last = nc.vector.tensor_scalar(win_tap[:, k * H + hh], win[:, hh], cw[:, hh, k:k + 1], 0.5,
                                                   ALU.mult, ALU.mult)
            last.then_inc(halves_ready, 1)
            front_xn(first_seq)
            for k in range(2):
                nc.vector.memset(outb[:, k], 0.0).then_inc(stored[k], 16)
            nc.vector.memset(rows[:], 0.0).then_inc(c_stored, 16)
            dve.wait_ge(split_hi, 1)
            nc.vector.tensor_tensor(conv_t[:, 1].rearrange("p k h c -> p (k h c)"),
                                    ps[:, 0:2].rearrange("p b c -> p (b c)"),
                                    conv_t[:, 0].rearrange("p k h c -> p (k h c)"), ALU.subtract).then_inc(split_lo, 1)
            front_xT_low("pro", None, first_seq)
            dve.wait_ge(ident_ready, 1)
            nc.vector.tensor_copy(ident16[:], ident[:])
            nc.vector.tensor_tensor(pick[:], ident[:, 0:BC], ident[:, BC:2 * BC], ALU.add)
            nc.vector.drain()
            nc.vector.tensor_tensor(pick[:], pick[:], ident[:, 2 * BC:3 * BC], ALU.add)
            nc.vector.drain()
            nc.vector.tensor_copy(pick_b[:], pick[0:STACK, 0:N].unsqueeze(2).broadcast_to([STACK, N, P]))
            nc.vector.tensor_copy(pick_g[:], pick[0:STACK].unsqueeze(2).broadcast_to([STACK, E, F])).then_inc(tables_ready, 1)
            dve.wait_ge(w_in, 16 * LOADS)
            nc.vector.tensor_copy(dtw_pad[:, :, STACK:], dtw[:]).then_inc(pads_ready, 1)
            nc.vector.tensor_scalar(cb_half[:], cb[:], 0.5, None, ALU.mult)
            nc.vector.tensor_scalar(glb_half[:], glb[:, 1:2], 0.5, None, ALU.mult)
            dve.wait_ge(a_exp_ready, 1)
            nc.vector.tensor_scalar(a_neg[:], a_neg[:], -1.0, None, ALU.mult).then_inc(small_ready, 1)
            for hh in range(H):
                nc.vector.tensor_scalar(diag_d[:, hh], ident[:], dsk[:, hh:hh + 1], None, ALU.mult)
            dve.wait_ge(experts_in, 32)
            nc.vector.tensor_copy(key_t[:, 0], key_sb[:])
            nc.vector.drain()
            nc.vector.tensor_tensor(key_t[:, 1], key_sb[:], key_t[:, 0], ALU.subtract).then_inc(tables_ready, 1)
            front_xc("pro", None, first_seq)
            dve.wait_ge(split_hi, 2)
            nc.vector.scalar_tensor_tensor(wz_t[:, 1], ps[:, 2, 0:2 * P], 0.5, wz_t[:, 0], ALU.mult, ALU.subtract)
            nc.vector.tensor_tensor(sel_t[:, 1], ps[:, 6, P:P + E], sel_t[:, 0], ALU.subtract).then_inc(split_lo, 1)
            front_bc("pro", None, first_seq)
            front_bc_low(first_seq)
            front_round(first_seq)
            front_gates("pro", None)
            front_sz("pro", None, first_seq, 0)
            front_sz("pro", None, first_seq, 1)
            front_dt(first_seq)

            def pieces(stage, s, at):
                if stage != "first":
                    if at == AT_DVE["yz"]:
                        back_yz(before(s))
                    if at == AT_DVE["glu"]:
                        back_glu(stage, s)
                    if at == AT_DVE["fin"]:
                        back_out(stage, s, before(s))
                if stage != "last":
                    if at == AT_DVE["stats"]:
                        front_stats(after(s))
                    if at == AT_DVE["xn"]:
                        front_xn(after(s))
                    if at == AT_DVE["xT"]:
                        front_xT_low(stage, s, after(s))
                    if at == AT_DVE["gates"]:
                        front_gates(stage, s)
                    if at == AT_DVE["xc"]:
                        front_xc(stage, s, after(s))
                    if at == AT_DVE["bc"]:
                        front_bc(stage, s, after(s))
                    if at == AT_DVE["bc_low"]:
                        front_bc_low(after(s))
                    if at == AT_DVE["round"]:
                        front_round(after(s))
                    for part in range(2):
                        if at == AT_DVE[f"z{part}"]:
                            front_sz(stage, s, after(s), part)
                    if at == AT_DVE["dt"]:
                        front_dt(after(s))

            def body(stage, s):
                for i in range(N):
                    n = s.b * N + i + 1
                    pieces(stage, s, 3 * i)
                    dve.wait_ge(b_ready, n)
                    if i == 0:
                        dve.wait_ge(dtu_ready, s.b + 1)
                    if stage != "first" or i >= 1:
                        dve.wait_ge(scan_done, n - 1)
                    low = 1 - i % 2
                    if low:
                        b_row = ps[:, 2].unsqueeze(1).broadcast_to([P, H, L])
                        nc.vector.tensor_tensor(ps[:, 1:3], dtu[:, s.par], b_row, ALU.mult).then_inc(dbu_ready, 1)
                    else:
                        nc.vector.tensor_tensor(ps[:, 1], dtu[:, s.par, 1], ps[:, 0], ALU.mult)
                        nc.vector.tensor_tensor(ps[:, 0], dtu[:, s.par, 0], ps[:, 0], ALU.mult).then_inc(dbu_ready, 1)
                    pieces(stage, s, 3 * i + 1)
                    dve.wait_ge(da_ready, n)
                    if stage != "first" or i >= 2:
                        dve.wait_ge(hc_ready, n - 2)
                    dve.wait_ge(dbu_ready, n)
                    nc.vector.tensor_tensor_scan(h[:, i % 2].rearrange("p h t -> p (h t)"),
                                                 dA[:, i % 2].rearrange("p h t -> p (h t)"),
                                                 ps[:, low:low + 2].rearrange("p h t -> p (h t)"), 0.0, ALU.mult,
                                                 ALU.add).then_inc(scan_done, 1)
                    pieces(stage, s, 3 * i + 2)

            walk(dve, body)
            back_yz(last_seq)
            back_glu("epi", None)
            back_out("epi", None, last_seq)

        @block.tensor
        def _(pe):
            def turn(dst, src, start=True, **more):
                return nc.tensor.matmul(dst, src, ident[0:src.shape[0], 0:src.shape[0]], is_transpose=True,
                                        start=start, stop=True, **more)

            def take(stage, now, job):
                k, n = ring(stage, now, job)
                if stage != "pro" or n > 1:
                    pe.wait_ge(emptied[k], n - 1)
                return k

            def split_products(out, weights, moving):
                for n, (a, b) in enumerate(((0, 0), (0, 1), (1, 0))):
                    last = nc.tensor.matmul(out, weights(a), moving(b), start=(n == 0), stop=(n == 2))
                return last

            def front_xT(stage, now, s):
                pe.wait_ge(xn_ready, s.b + 1)
                for job, src in (("xnT", xn), ("xn2T", xn2)):
                    k = take(stage, now, job)
                    for j in range(T):
                        last = turn(ps[:, RING + k, j * P:(j + 1) * P], src[:, j])
                    last.then_inc(filled[k], 1)

            def front_logits(stage, now, s):
                wait_emptied(pe, stage, now, "xnT")
                k = take(stage, now, "logits")
                for j in range(T):
                    last = split_products(ps[:, RING + k, j * E:(j + 1) * E],
                                          lambda a: xnT[:, s.par, a, j * P:(j + 1) * P], lambda b: sel_t[:, b])
                last.then_inc(filled[k], 1)

            def front_conv(stage, now, s, part):
                hh, start = part // 2, part % 2 * L // 2
                if part == 0:
                    pe.wait_ge(xn2T_low, s.b + 1)
                k = take(stage, now, f"conv{part}")
                for tap in range(TAPS):
                    for a, b in ((0, 0), (0, 1), (1, 0)):
                        last = nc.tensor.matmul(ps[:, RING + k, 0:L // 2], conv_t[:, a, tap, hh],
                                                xn2T[:, b, start + tap:start + tap + L // 2],
                                                start=(tap + a + b == 0), stop=(tap + a == TAPS))
                last.then_inc(filled[k], 1)

            def front_z(stage, now, part):
                k = take(stage, now, f"z{part}")
                for j in range(2):
                    at = TAPS - 1 + (2 * part + j) * P
                    last = split_products(ps[:, RING + k, j * H * P:(j + 1) * H * P],
                                          lambda a: xn2T[:, a, at:at + P], lambda b: wz_t[:, b])
                last.then_inc(filled[k], 1)

            def front_xdbl(stage, now, s):
                pe.wait_ge(xc_ready, s.b + 1)
                k = take(stage, now, "xdbl")
                for hh in range(H):
                    last = nc.tensor.matmul(ps[0:STACK + R, RING + k], xp_t[:, hh], xc[:, hh], start=(hh == 0),
                                            stop=(hh == H - 1))
                last.then_inc(filled[k], 1)

            def front_gT(stage, now, s):
                pe.wait_ge(g3_ready, s.b + 1)
                k = take(stage, now, "gT")
                for j in range(T):
                    last = nc.tensor.matmul(ps[0:STACK, RING + k, j * P // 2:(j + 1) * P // 2].bitcast(bf16), g3[:, j],
                                            ident16[:], is_transpose=True, start=True, stop=True)
                last.then_inc(filled[k], 1)

            def front_dt(stage, now, s):
                pe.wait_ge(dtr_ready, s.b + 1)
                for hh in range(H):
                    k = take(stage, now, f"dt{hh}")
                    nc.tensor.matmul(ps[:, RING + k], dtw_t[STACK:STACK + R, hh], dtr,
                                     start=True, stop=True).then_inc(filled[k], 1)

            def back_yT(stage, now, s):
                pe.wait_ge(yz_ready, s.b + 1)
                for hh in range(H):
                    k = take(stage, now, f"yT{hh}")
                    for j in range(T):
                        last = turn(ps[:, RING + k, j * P:(j + 1) * P], yz[:, j, hh * P:(hh + 1) * P])
                    last.then_inc(filled[k], 1)

            def back_m(stage, now):
                wait_emptied(pe, stage, now, "yT1")
                k = take(stage, now, "m")
                for hh in range(H):
                    last = nc.tensor.matmul(ps[:, RING + k], ow_t[:, hh], yT[:, hh], start=(hh == 0), stop=(hh == H - 1))
                last.then_inc(filled[k], 1)

            def back_glu(stage, now):
                wait_emptied(pe, stage, now, "m")
                for r in (1, 0):
                    k = take(stage, now, f"g{r}")
                    nc.tensor.matmul(ps[:, RING + k], gw_t[:, r], mg[:], start=True, stop=True).then_inc(filled[k], 1)

            def back_fin(stage, now, s):
                wait_emptied(pe, stage, now, "g0")
                pe.wait_ge(moe_s_ready, s.b + 1)
                for part in range(2):
                    k = take(stage, now, f"fin{part}")
                    for j in range(2):
                        at = slice((2 * part + j) * P, (2 * part + j + 1) * P)
                        turn(ps[:, RING + k, j * P:(j + 1) * P], moe_s[:, at])
                        last = turn(ps[:, RING + k, j * P:(j + 1) * P], m2[:, at], start=False,
                                    skip_group_check=True)
                    last.then_inc(filled[k], 1)

            def sum_y(stage, s, i):
                if i == 0:
                    if stage != "first":
                        pe.wait_ge(yz_ready, s.b)
                    for j in range(T):
                        for hh in range(H):
                            nc.tensor.matmul(ps[:, YACC + j // 2, (j % 2 * H + hh) * P:(j % 2 * H + hh + 1) * P],
                                             xc[:, hh, j * P:(j + 1) * P], diag_d[:, hh], start=(j % 2 + hh == 0),
                                             stop=False, skip_group_check=True)
                pe.wait_ge(hc_ready, s.b * N + i + 1)
                for j in range(T):
                    for hh in range(H):
                        last = turn(ps[:, YACC + j // 2, (j % 2 * H + hh) * P:(j % 2 * H + hh + 1) * P],
                                    hC[:, i % 4, hh, j * P:(j + 1) * P], start=False, skip_group_check=True)
                last.then_inc(y_done, 1)

            def sum_moe(stage, s, i):
                if i == 0 and stage != "first":
                    pe.wait_ge(moe_s_ready, s.b)
                pe.wait_ge(hg_ready, s.b * N + i + 1)
                nc.tensor.matmul(ps[:, MOE], val_sb[:, i], hg[:, i % 2], start=(i == 0),
                                 stop=(i == N - 1)).then_inc(moe_done, 1)

            def spread_b(s, i, n, reused=True):
                if i == 0:
                    pe.wait_ge(bc_ready, s.b + 1)
                if reused:
                    pe.wait_ge(scan_done, n - 2)
                nc.tensor.matmul(ps[:, 2 - i % 2 * 2], pick_b[:, i], bc3[:, s.par], start=True,
                                 stop=True).then_inc(b_ready, 1)

            pe.wait_ge(ident_ready, 1)
            pe.wait_ge(halves_ready, 1)
            for k in range(TAPS):
                for hh in range(H):
                    at = (k % 2 * H + hh) * P
                    last = turn(ps[:, k // 2, at:at + P], win_tap[:, k * H + hh])
                if k % 2:
                    last.then_inc(prep_pe, 1)
            front_xT("pro", None, first_seq)
            pe.wait_ge(split_lo, 1)
            for part in range(CONVS):
                front_conv("pro", None, first_seq, part)
            pe.wait_ge(w_in, 16 * LOADS)
            for hh in range(H):
                turn(ps[:, 2, hh * P:(hh + 1) * P], win[:, H + hh])
                last = turn(ps[:, 2, (H + hh) * P:(H + hh + 1) * P], ow[:, hh * P:(hh + 1) * P])
            last.then_inc(prep_pe, 1)
            pe.wait_ge(pads_ready, 1)
            for hh in range(H):
                turn(ps[:, 5, hh * P:(hh + 1) * P], gw[:, hh])
                last = turn(ps[0:STACK + R, 5, (H + hh) * P:(H + hh + 1) * P], dtw_pad[:, hh])
            last.then_inc(prep_pe, 1)
            for hh in range(H):
                turn(ps[:, 6, hh * (R + BC):(hh + 1) * (R + BC)], xpw[:, hh * P:(hh + 1) * P])
            turn(ps[:, 6, P:P + E], selw[:]).then_inc(prep_pe, 1)
            pe.wait_ge(split_hi, 2)
            front_xdbl("pro", None, first_seq)
            pe.wait_ge(split_lo, 2)
            front_logits("pro", None, first_seq)
            front_dt("pro", None, first_seq)
            pe.wait_ge(tables_ready, 1)
            spread_b(first_seq, 0, 1, reused=False)
            front_z("pro", None, 0)
            front_z("pro", None, 1)
            front_gT("pro", None, first_seq)

            pe.wait_ge(tables_ready, 2)
            def pieces(stage, s, at):
                if stage != "first":
                    if at == AT["yT"]:
                        back_yT(stage, s, before(s))
                    if at == AT["m"]:
                        back_m(stage, s)
                    if at == AT["glu"]:
                        back_glu(stage, s)
                    if at == AT["fin"]:
                        back_fin(stage, s, before(s))
                if stage != "last":
                    if at == AT["xT"]:
                        front_xT(stage, s, after(s))
                    if at == AT["logits"]:
                        front_logits(stage, s, after(s))
                    for part in range(CONVS):
                        if at == AT[f"conv{part}"]:
                            front_conv(stage, s, after(s), part)
                    if at == AT["xdbl"]:
                        front_xdbl(stage, s, after(s))
                    if at == AT["dt"]:
                        front_dt(stage, s, after(s))
                    for part in range(2):
                        if at == AT[f"z{part}"]:
                            front_z(stage, s, part)
                    if at == AT["gT"]:
                        front_gT(stage, s, after(s))

            def body(stage, s):
                for i in range(N):
                    n = s.b * N + i + 1
                    if i < N - 1:
                        spread_b(s, i + 1, n + 1, reused=stage != "first" or i >= 1)
                    elif stage != "last":
                        spread_b(after(s), 0, n + 1)
                    pieces(stage, s, 3 * i)
                    if i >= Y_LAG:
                        sum_y(stage, s, i - Y_LAG)
                    elif stage != "first":
                        sum_y(stage, before(s), N + i - Y_LAG)
                    k = take(stage, s, f"S{i}")
                    split_products(ps[:, RING + k],
                                   lambda a: key_t[:, a, 2 * i:2 * i + 2].rearrange("p e f -> p (e f)"),
                                   lambda b: xnT[:, s.par, b]).then_inc(filled[k], 1)
                    pieces(stage, s, 3 * i + 1)
                    if i >= MOE_LAG:
                        sum_moe(stage, s, i - MOE_LAG)
                    elif stage != "first":
                        sum_moe(stage, before(s), N + i - MOE_LAG)
                    k = take(stage, s, f"G{i}")
                    if i == 0:
                        if stage == "first":
                            wait_emptied(pe, "pro", None, "gT")
                        else:
                            wait_emptied(pe, stage, s, "gT", ago=1)
                    nc.tensor.matmul(ps[:, RING + k], pick_g[:, 2 * i:2 * i + 2].rearrange("p e f -> p (e f)"),
                                     gT[:, s.par], start=True, stop=True).then_inc(filled[k], 1)
                    pieces(stage, s, 3 * i + 2)

            walk(pe, body)
            for i in range(N - Y_LAG, N):
                sum_y("last", last_seq, i)
            for i in range(N - MOE_LAG, N):
                sum_moe("last", last_seq, i)
            back_yT("epi", None, last_seq)
            back_m("epi", None)
            back_glu("epi", None)
            back_fin("epi", None, last_seq)


_INS = ["L0_attn_x", "L0_attn_ln_g", "L0_attn_ln_b", "L0_attn_in_proj_w", "L0_attn_conv_w", "L0_attn_conv_b",
        "L0_attn_x_proj_w", "L0_attn_dt_proj_w", "L0_attn_dt_proj_b", "L0_attn_A_log", "L0_attn_D",
        "L0_attn_out_proj_w", "L0_attn_glu_w", "L0_attn_glu_b", "L0_ffn_expert_sel", "L0_ffn_keys", "L0_ffn_values"]


def kernel(**inputs):
    import numpy as _np
    import concourse.bacc as _bacc
    from concourse import mybir as _mybir
    from concourse.bass_utils import run_bass_kernel_spmd as _run

    nc = _bacc.Bacc("TRN2", target_bir_lowering=False, num_devices=1)
    arrays, args = {}, []
    for name in _INS:
        a = _np.ascontiguousarray(inputs[name])
        arrays[f"in_{name}_dram"] = a
        args.append(nc.dram_tensor(f"in_{name}_dram", a.shape, _mybir.dt.from_np(a.dtype), kind="ExternalInput").ap())
    shape = inputs["L0_attn_x"].shape
    args.append(nc.dram_tensor("out_dram", shape, _mybir.dt.float32, kind="ExternalOutput").ap())
    mamba_moe(nc, *args)
    r = _run(nc, [arrays], core_ids=[0])
    return r.results[0]["out_dram"]
```
